# Optimizing a Trainium2 kernel written in Bass

```python
import numpy as np
import jax
import jax.numpy as jnp

def _softmax(x, axis=-1):
    return jax.nn.softmax(x, axis=axis)

def _gelu(x):
    return jax.nn.gelu(x, approximate=True)

def _silu(x):
    return jax.nn.silu(x)

def _sigmoid(x):
    return jax.nn.sigmoid(x)

def _layernorm(x, axis=-1, eps=1e-05):
    m = jnp.mean(x, axis=axis, keepdims=True)
    v = jnp.var(x, axis=axis, keepdims=True)
    return (x - m) / jnp.sqrt(v + eps)

def _scatter_add(tgt, idx, src, axis=0):
    return tgt.at[idx].add(src)

def _segment_sum(src, seg, n):
    return jax.ops.segment_sum(src, seg, n)
kernel_name = 'mk_adj_resnorm_d2_adj_r2_282e44'

def setup_inputs(seed: int=0):
    np.random.seed(seed)
    _w = jnp.asarray

    def _rec_inputs():
        import jax
        import jax.numpy as jnp
        _gk = jax.random.key(seed)
        x = -0.0002928 + 1 * jax.random.normal(jax.random.fold_in(_gk, 1), (8, 1024, 128), jnp.float32)
        _a = jax.random.bernoulli(jax.random.fold_in(_gk, 2), 0.00390625, (1024, 1024))
        _a = jnp.logical_or(_a, jnp.swapaxes(_a, -1, -2))
        _a = jnp.logical_or(_a, jnp.eye(1024, dtype=bool))
        _af = _a.astype(jnp.float32)
        _af = _af * jax.random.uniform(jax.random.fold_in(_gk, 3), (1024, 1024), jnp.float32, 0.05, 1)
        adj = _af
        return (x, adj)
    x, adj = _rec_inputs()

    def _L0_gnn_setup():
        import jax, jax.numpy as jnp
        import numpy as np
        N = 2048
        NFEAT, NHID, NCLASS = (128, 256, 128)
        B = 4

        def _slconv(x, adj, S, W):
            support = jnp.einsum('bnf,fh->bnh', x, W)
            weighting = adj * S
            return jnp.einsum('nm,bmh->bnh', weighting, support)
        key = jax.random.key(seed)
        ks = jax.random.split(key, 6)
        x = jax.random.normal(ks[0], (B, N, NFEAT), dtype=jnp.float32)
        adj = jax.random.uniform(ks[1], (N, N), dtype=jnp.float32)
        S = jnp.ones((N, N), dtype=jnp.float32)
        W1 = jax.random.normal(ks[2], (NFEAT, NHID), dtype=jnp.float32) / np.sqrt(NFEAT)
        W2 = jax.random.normal(ks[3], (NHID, 2 * NHID), dtype=jnp.float32) / np.sqrt(NHID)
        W3 = jax.random.normal(ks[4], (2 * NHID, NCLASS), dtype=jnp.float32) / np.sqrt(2 * NHID)
        return {'x': x, 'adj': adj, 'S': S, 'W1': W1, 'W2': W2, 'W3': W3}
    _L0_gnn_all = _L0_gnn_setup()
    _L0_gnn_in = {k: v for k, v in _L0_gnn_all.items() if k in ('W1', 'W2', 'W3')}
    del _L0_gnn_all

    def _L1_gnn_setup():
        import jax, jax.numpy as jnp
        import numpy as np
        B, T, D, H = (64, 1024, 128, 128)
        MAX_SKIP = 4

        def _lstm_last(Wih, Whh, bih, bhh, xs):
            N, _, Hd = xs.shape
            bias = bih + bhh

            def step(carry, x_t):
                h, c = carry
                g = x_t @ Wih.T + h @ Whh.T + bias
                i, f, gg, o = jnp.split(g, 4, axis=-1)
                c = jax.nn.sigmoid(f) * c + jax.nn.sigmoid(i) * jnp.tanh(gg)
                h = jax.nn.sigmoid(o) * jnp.tanh(c)
                return ((h, c), None)
            init = (jnp.zeros((N, Hd), xs.dtype), jnp.zeros((N, Hd), xs.dtype))
            (h_last, _), _ = jax.lax.scan(step, init, jnp.swapaxes(xs, 0, 1))
            return h_last
        key = jax.random.key(seed)
        ks = jax.random.split(key, 8)
        s = 0.05
        x = jax.random.normal(ks[0], (B, T, D), jnp.float32)
        adj = jax.random.uniform(ks[1], (T, T), jnp.float32) / T
        Wg0 = jax.random.normal(ks[2], (D, H), jnp.float32) * s
        bg0 = jnp.zeros((H,), jnp.float32)
        Wg1 = jax.random.normal(ks[3], (H, H), jnp.float32) * s
        bg1 = jnp.zeros((H,), jnp.float32)
        Wih = jax.random.normal(ks[4], (MAX_SKIP, 4 * H, H), jnp.float32) * s
        Whh = jax.random.normal(ks[5], (MAX_SKIP, 4 * H, H), jnp.float32) * s
        bih = jax.random.normal(ks[6], (MAX_SKIP, 4 * H), jnp.float32) * s
        bhh = jax.random.normal(ks[7], (MAX_SKIP, 4 * H), jnp.float32) * s
        return dict(x=x, adj=adj, Wg0=Wg0, bg0=bg0, Wg1=Wg1, bg1=bg1, Wih=Wih, Whh=Whh, bih=bih, bhh=bhh)
    _L1_gnn_all = _L1_gnn_setup()
    _L1_gnn_in = {k: v for k, v in _L1_gnn_all.items() if k in ('Wg0', 'bg0', 'Wg1', 'bg1', 'Wih', 'Whh', 'bih', 'bhh')}
    del _L1_gnn_all
    return {'x': x, 'adj': adj, 'L0_gnn_W1': _L0_gnn_in['W1'], 'L0_gnn_W2': _L0_gnn_in['W2'], 'L0_gnn_W3': _L0_gnn_in['W3'], 'L1_gnn_Wg0': _L1_gnn_in['Wg0'], 'L1_gnn_bg0': _L1_gnn_in['bg0'], 'L1_gnn_Wg1': _L1_gnn_in['Wg1'], 'L1_gnn_bg1': _L1_gnn_in['bg1'], 'L1_gnn_Wih': _L1_gnn_in['Wih'], 'L1_gnn_Whh': _L1_gnn_in['Whh'], 'L1_gnn_bih': _L1_gnn_in['bih'], 'L1_gnn_bhh': _L1_gnn_in['bhh']}

def reference(x, adj, L0_gnn_W1, L0_gnn_W2, L0_gnn_W3, L1_gnn_Wg0, L1_gnn_bg0, L1_gnn_Wg1, L1_gnn_bg1, L1_gnn_Wih, L1_gnn_Whh, L1_gnn_bih, L1_gnn_bhh):
    import jax
    import jax.numpy as jnp

    def _L0_gnn_ref(x, adj, S, W1, W2, W3):
        import jax, jax.numpy as jnp
        import numpy as np
        N = 2048
        NFEAT, NHID, NCLASS = (128, 256, 128)
        B = 4

        def _slconv(x, adj, S, W):
            support = jnp.einsum('bnf,fh->bnh', x, W)
            weighting = adj * S
            return jnp.einsum('nm,bmh->bnh', weighting, support)
        h = jax.nn.relu(_slconv(x, adj, S, W1))
        h = jax.nn.relu(_slconv(h, adj, S, W2))
        return _slconv(h, adj, S, W3)

    def _L1_gnn_ref(x, adj, Wg0, bg0, Wg1, bg1, Wih, Whh, bih, bhh):
        import jax, jax.numpy as jnp
        import numpy as np
        B, T, D, H = (64, 1024, 128, 128)
        MAX_SKIP = 4

        def _lstm_last(Wih, Whh, bih, bhh, xs):
            N, _, Hd = xs.shape
            bias = bih + bhh

            def step(carry, x_t):
                h, c = carry
                g = x_t @ Wih.T + h @ Whh.T + bias
                i, f, gg, o = jnp.split(g, 4, axis=-1)
                c = jax.nn.sigmoid(f) * c + jax.nn.sigmoid(i) * jnp.tanh(gg)
                h = jax.nn.sigmoid(o) * jnp.tanh(c)
                return ((h, c), None)
            init = (jnp.zeros((N, Hd), xs.dtype), jnp.zeros((N, Hd), xs.dtype))
            (h_last, _), _ = jax.lax.scan(step, init, jnp.swapaxes(xs, 0, 1))
            return h_last
        h = jax.nn.relu(jnp.einsum('ts,bsh->bth', adj, x @ Wg0 + bg0))
        h = jax.nn.relu(jnp.einsum('ts,bsh->bth', adj, h @ Wg1 + bg1))
        Bv, Tv, Hd = h.shape
        for p in range(1, MAX_SKIP + 1):
            nw = Tv // p
            wins = h[:, :nw * p, :].reshape(Bv * nw, p, Hd)
            last = _lstm_last(Wih[p - 1], Whh[p - 1], bih[p - 1], bhh[p - 1], wins)
            idx = jnp.arange(nw) * p + (p - 1)
            h = h.at[:, idx, :].set(last.reshape(Bv, nw, Hd))
        return h
    x = _layernorm(x + _L0_gnn_ref(x, adj, adj, L0_gnn_W1, L0_gnn_W2, L0_gnn_W3), axis=-1)
    x = _layernorm(x + _L1_gnn_ref(x, adj, L1_gnn_Wg0, L1_gnn_bg0, L1_gnn_Wg1, L1_gnn_bg1, L1_gnn_Wih, L1_gnn_Whh, L1_gnn_bih, L1_gnn_bhh), axis=-1)
    return x

_drawn_inputs = setup_inputs


def setup_inputs(seed=0):
    import zlib

    import numpy as np

    out = dict(_drawn_inputs(seed))
    spreads = {'L1_gnn_bg0': (0.0, 0.1), 'L1_gnn_bg1': (0.0, 0.487)}
    factors = {'L1_gnn_Whh': 8.0, 'L1_gnn_bih': 3.003, 'L1_gnn_bhh': 3.059}
    for name, (base, spread) in spreads.items():
        noise = np.random.default_rng([zlib.crc32(name.encode()), seed]).standard_normal(out[name].shape)
        drawn = base * np.exp(spread * noise) if base else spread * noise
        out[name] = jnp.asarray(drawn.astype(out[name].dtype))
    for name, factor in factors.items():
        out[name] = (out[name] * factor).astype(out[name].dtype)
    return out
```

```python
from contextlib import ExitStack

import numpy as np

import concourse.bass as bass
import concourse.mybir as mybir

F32 = mybir.dt.float32
F32R = mybir.dt.float32r
I32 = mybir.dt.int32
ALU = mybir.AluOpType
ACT = mybir.ActivationFunctionType

P = 128
BANK = 512
BANKS = 8
HI, LO = 0, 1
EPS = 1e-5
NEWTON = 3
RSQRT_OWN = 3 + 3 * NEWTON
SKIPS = 4
GI, GF, GG, GO = range(4)


def build(nc, x, adj_t, w1, w2, w3, wg0, bg0, wg1, bg1, wih_t, whh_t, bih, bhh, out):
    B, N, F = x.shape
    H1, H2 = w1.shape[1], w2.shape[1]
    MT = N // P
    HALVES = N // BANK
    K2, K3 = H1 // P, H2 // P
    PAIRS = B // 2
    G4 = SKIPS * P
    assert F == P and HALVES == 2 and w3.shape[1] == F and wih_t.shape == (SKIPS, F, 4 * F)

    ctx = ExitStack()
    with ctx:
        base = (nc.sbuf_base + 63) // 64 * 64
        top = [base]

        def place(nbytes):
            at = top[0]
            top[0] += (nbytes + 63) // 64 * 64
            return at

        def sb(name, shape, dt, at=None):
            size = 4 * int(np.prod(shape[1:]))
            return nc.alloc_sbuf_tensor_at(name, shape, dt, offset=place(size) if at is None else at)

        KB = 1024
        adj_at = place(2 * MT * N * 4)
        adj = sb("adj", [P, 2, MT, N], F32R, adj_at)
        square = sb("square", [P, MT, N], F32, adj_at + MT * N * 4)
        xb = sb("xb", [P, B, MT, F], F32)
        node = sb("node", [P, 2, N], F32R)
        big_at = place(32 * KB)
        y1 = sb("y1", [P, 2, N], F32R, big_at)
        h1 = sb("h1", [P, 2, MT, H1], F32R, big_at + 8 * KB)
        h2 = sb("h2", [P, 2, K3, N], F32R, big_at)
        adj_raw = sb("adj_raw", [P, MT, N], F32, big_at)
        lw = sb("lw", [P, 2, 2 * SKIPS - 1, G4], F32R, big_at)
        rowsum = sb("rowsum", [P, N], F32R, big_at + 28 * KB)
        r2_at = place(16 * KB)
        y2 = sb("y2", [P, 2, K2, N], F32R, r2_at)
        w0_raw = sb("w0_raw", [P, H1 + K2 * H2 + K3 * F], F32, r2_at)
        z = sb("z", [P, 2, N], F32R, r2_at)
        hs_at = r2_at + 8 * KB
        HTW = N + 2
        ht = sb("ht", [P, 2, 2, HTW], F32R, hs_at)
        r3_at = place(16 * KB)
        s3 = sb("s3", [P, 2, MT, 2, F], F32R, r3_at)
        w0_at = place(4 * 2 * (H1 + K2 * H2 + K3 * F))
        w1s = sb("w1s", [P, 2, H1], F32R, w0_at)
        w2s = sb("w2s", [P, 2, K2, H2], F32R, w0_at + 8 * H1)
        w3s = sb("w3s", [P, K3, 2, F], F32R, w0_at + 8 * (H1 + K2 * H2))
        lw_raw_at = place(4 * (2 * SKIPS - 1) * G4)
        lw_raw = sb("lw_raw", [P, 2 * SKIPS - 1, G4], F32, lw_raw_at)
        gates_at = (hs_at + 4 * 4 * HTW + 63) // 64 * 64
        gates = sb("gates", [P, 2, 5, BANK], F32, gates_at)
        hstep = sb("hstep", [P, 2, 2, BANK], F32R, gates_at + 4 * 10 * BANK)
        assert gates_at + 4 * 14 * BANK <= top[0]
        wg_raw = sb("wg_raw", [P, 4, F], F32)
        wgs = sb("wgs", [P, 2, 2, F], F32R)
        cross_at = place(2 * KB)
        cross = sb("cross", [P, 2, 2, F], F32, cross_at)
        bparts = sb("bparts", [P, 2, 2, F], F32R, cross_at)
        brow = sb("brow", [P, 2, F], F32R)
        ident_f = sb("ident_f", [P, P], F32)
        ident = sb("ident", [P, P], F32R)
        ones = sb("ones", [P, P], F32R)
        lb_raw = sb("lb_raw", [P, 2, SKIPS * 4], F32)
        lb = sb("lb", [P, SKIPS * 4], F32)
        sel = sb("sel", [P, 4], F32)
        s3full = sb("s3full", [P, 2, F], F32)
        stats = sb("stats", [P, 16, 6], F32)
        mv = sb("mv", [P, 16, 2], F32)
        warm = sb("warm", [P, 1], F32)
        took_wait = sb("took_wait", [P, 1], F32)
        newton = sb("newton", [P, 3, 16], F32)
        assert top[0] <= nc.sbuf_usable_end

        ps = ctx.enter_context(nc.psum_tensor("ps", [P, BANKS, BANK], F32))

        def sem(name):
            return ctx.enter_context(nc.semaphore(name))

        x0_in = sem("x0_in")
        xr_in = sem("xr_in")
        adj_in = [sem(f"adj_in{m}") for m in range(MT)]
        w0_in = sem("w0_in")
        lw_in = sem("lw_in")
        eye_set = sem("eye_set")
        const_set = sem("const_set")
        own = sem("own")
        sq_done = sem("sq_done")
        a_mm, a_hi, a_lo = sem("a_mm"), sem("a_hi"), sem("a_lo")
        a_ln = sem("a_ln")
        b_mm, b_hi, b_lo = sem("b_mm"), sem("b_hi"), sem("b_lo")
        gate_mm = sem("gate_mm")
        gate_act = sem("gate_act")
        cell_done = sem("cell_done")
        tanh_done = sem("tanh_done")
        h_done = sem("h_done")
        fin_mm = sem("fin_mm")
        fin_add = sem("fin_add")
        out_ready = sem("out_ready")
        out_done = sem("out_done")

        A1, P1, A2, P2, P3, A3 = HALVES, MT * H1 // BANK, HALVES * K2, HALVES * K3, MT // 2, MT // 2
        A_MM = A1 + P1 + A2 + P2 + P3
        A_LO = A_MM + 1
        A_MM_PAIR, A_LO_PAIR = 2 * A_MM + A3, 2 * A_LO + A3
        A_HI_PAIR = 2 * A_LO
        A_PRE = 1 + MT + 1
        assert A_MM_PAIR % BANKS == 0

        def a_lo_of(q):
            if q < 0:
                return a_lo_of(q + A_MM_PAIR) - A_LO_PAIR
            if q >= 2 * A_MM:
                return 2 * A_LO + (q - 2 * A_MM) + 1
            j, r = divmod(q, A_MM)
            return j * A_LO + r + 1 + (r >= A1 + P1 + A2)

        B_MM = 8
        B_LO = B_MM + 1
        LW = 2 * SKIPS - 1
        B_PRE = MT + 1 + LW
        assert B_MM == BANKS

        def b_lo_of(r):
            return r + 1 + (r >= 6)

        STEPS = [(1, 0, 0), (1, 0, BANK)] + [(p, s, s) for p in range(2, SKIPS + 1) for s in range(p)]
        LUNITS = 2 * len(STEPS)

        def windows(p):
            n = min(N // p, BANK)
            return n, n + n % 2

        def gates_of(s):
            return (GI, GG, GO) if s == 0 else (GI, GG, GF, GO)

        GATE0 = [0]
        for _, s, _ in STEPS:
            for _ in range(2):
                GATE0.append(GATE0[-1] + len(gates_of(s)))
        GATES = GATE0[LUNITS]

        GATE_PRE = FIN_PRE = 1

        def whh(p):
            return SKIPS + p - 2

        def f32(ap):
            return ap.bitcast(F32)

        block = ctx.enter_context(nc.Block())

        @block.sync
        def _(sp):
            sp.dma_start(xb[:, 0], x[0].rearrange("(t p) c -> p t c", p=P)).then_inc(x0_in, 16)
            for m in range(MT):
                sp.dma_start(square[:, m, :], adj_t[m * P:(m + 1) * P, :]).then_inc(adj_in[m], 16)
            sp.dma_start(w0_raw[:, 0:H1], w1).then_inc(w0_in, 16)
            sp.dma_start(w0_raw[:, H1:H1 + K2 * H2].rearrange("p (k g) -> p k g", k=K2),
                         w2.rearrange("(k p) g -> p k g", p=P)).then_inc(w0_in, 16)
            sp.dma_start(w0_raw[:, H1 + K2 * H2:].rearrange("p (k g) -> p k g", k=K3),
                         w3.rearrange("(k p) g -> p k g", p=P)).then_inc(w0_in, 16)
            for b in range(1, B):
                sp.dma_start(xb[:, b], x[b].rearrange("(t p) c -> p t c", p=P)).then_inc(xr_in, 16)
            for k, small in enumerate((wg0, wg1, bg0, bg1)):
                sp.dma_start(wg_raw[:, k, :], small).then_inc(lw_in, 16)
            sp.dma_start(lb_raw[:, 0, :], bih).then_inc(lw_in, 16)
            sp.dma_start(lb_raw[:, 1, :], bhh).then_inc(lw_in, 16)
            sp.dma_start(lw_raw[:, 0:SKIPS, :], wih_t.rearrange("s f g -> f s g")).then_inc(lw_in, 16)
            sp.dma_start(lw_raw[:, SKIPS:, :], whh_t[1:].rearrange("s f g -> f s g")).then_inc(lw_in, 16)
            sp.wait_ge(a_mm, PAIRS * A_MM_PAIR - A3)
            for m in range(MT):
                sp.dma_start(adj_raw[:, m, :], adj_t[m * P:(m + 1) * P, :]).then_inc(adj_in[m], 16)
            with sp.Fori(0, PAIRS) as it:
                for j in range(2):
                    sp.wait_ge(out_ready, it * 2 + (j + 1))
                    sp.dma_start(out[bass.ds(it * 2 + j, 1)].rearrange("b (t p) c -> p (b t) c", p=P),
                                 xb[:, bass.ds(it * 2 + j, 1)].rearrange("p b t c -> p (b t) c")
                                 ).then_inc(out_done, 16)
            sp.wait_ge(out_done, 16 * B)

        @block.gpsimd
        def _(pool):
            nc.gpsimd.memset(ident_f[:], 1.0).then_inc(eye_set, 1)
            pool.wait_ge(eye_set, 1)
            nc.gpsimd.affine_select(out=ident_f[:], in_=ident_f[:], compare_op=ALU.is_equal, fill=0.0,
                                    base=0, pattern=[[-1, P]], channel_multiplier=1).then_inc(eye_set, 1)

        @block.tensor
        def _(pe):
            def product(dst, stat, mov, start, stop):
                pe.matmul(dst, stat(HI), mov(HI), start=start, stop=False)
                pe.matmul(dst, stat(HI), mov(LO), start=False, stop=False)
                return pe.matmul(dst, stat(LO), mov(HI), start=False, stop=stop)

            def adj_by(dst, src, half, tile_ready=None):
                for m in range(MT):
                    if tile_ready is not None:
                        tile_ready(m)
                    last = product(dst, lambda i: src(i, m),
                                   lambda i: adj[:, i, m, half * BANK:(half + 1) * BANK], m == 0, m == MT - 1)
                return last

            with pe.Fori(0, PAIRS) as it:
                lo0 = it * A_LO_PAIR + A_PRE

                def bank_free(q):
                    pe.wait_ge(a_lo, lo0 + a_lo_of(q - BANKS))

                for j in range(2):
                    q = j * A_MM
                    if j == 0:
                        pe.wait_ge(a_lo, it * A_LO_PAIR + 1)
                    else:
                        pe.wait_ge(a_lo, lo0 + a_lo_of(A1 + P1 + A2 - 1) + 1)
                    for half in range(HALVES):
                        bank_free(q)

                        def tile_ready(m):
                            pe.wait_ge(a_lo, it * A_LO_PAIR + 1 + (m + 1))
                        adj_by(ps[:, q % BANKS, :], lambda i, m: node[:, i, m * P:(m + 1) * P], half,
                               tile_ready if j == 0 and half == 0 else None).then_inc(a_mm, 1)
                        q += 1
                    pe.wait_ge(a_lo, lo0)
                    per = BANK // H1
                    for u in range(P1):
                        bank_free(q)
                        pe.wait_ge(a_lo, lo0 + a_lo_of(j * A_MM + u * per * P // BANK))
                        for t in range(per):
                            nt = (u * per + t) * P
                            last = product(ps[:, q % BANKS, t * H1:(t + 1) * H1],
                                           lambda i: y1[:, i, nt:nt + P], lambda i: w1s[:, i, :], True, True)
                        last.then_inc(a_mm, 1)
                        q += 1
                    h1_unit = j * A_MM + A1
                    for half in range(HALVES):
                        for k in range(K2):
                            bank_free(q)

                            def h1_ready(m):
                                if m % per == 0:
                                    pe.wait_ge(a_lo, lo0 + a_lo_of(h1_unit + m // per))
                            adj_by(ps[:, q % BANKS, :], lambda i, m: h1[:, i, m, k * P:(k + 1) * P], half,
                                   h1_ready if half == 0 and k == 0 else None).then_inc(a_mm, 1)
                            q += 1
                    y2_unit = h1_unit + P1
                    for half in range(HALVES):
                        pe.wait_ge(a_lo, lo0 + a_lo_of(y2_unit + (half + 1) * K2 - 1))
                        for g in range(K3):
                            bank_free(q)
                            for k in range(K2):
                                last = product(ps[:, q % BANKS, :], lambda i: w2s[:, i, k, g * P:(g + 1) * P],
                                               lambda i: y2[:, i, k, half * BANK:(half + 1) * BANK],
                                               k == 0, k == K2 - 1)
                            last.then_inc(a_mm, 1)
                            q += 1
                    h2_unit = y2_unit + A2
                    for u in range(P3):
                        bank_free(q)
                        half = u * 2 * P // BANK
                        pe.wait_ge(a_lo, lo0 + a_lo_of(h2_unit + (half + 1) * K3 - 1))
                        for t in range(2):
                            nt = (2 * u + t) * P
                            for k in range(K3):
                                pe.matmul(ps[:, q % BANKS, 2 * t * F:(2 * t + 2) * F], h2[:, HI, k, nt:nt + P],
                                          w3s[:, k, :, :].rearrange("p a c -> p (a c)"),
                                          start=(k == 0), stop=False, skip_group_check=True)
                                last = pe.matmul(ps[:, q % BANKS, 2 * t * F:(2 * t + 1) * F],
                                                 h2[:, LO, k, nt:nt + P], w3s[:, k, HI, :],
                                                 start=False, stop=(k == K3 - 1), skip_group_check=True)
                        last.then_inc(a_mm, 1)
                        q += 1
                for u in range(A3):
                    bank_free(q)
                    if u == 0:
                        pe.wait_ge(a_lo, lo0 + a_lo_of(2 * A_MM - 1))
                    for t in range(2):
                        nt = (2 * u + t) * P
                        for m in range(MT):
                            last = product(ps[:, q % BANKS, 2 * t * F:(2 * t + 2) * F],
                                           lambda i: adj[:, i, m, nt:nt + P],
                                           lambda i: s3[:, i, m, :, :].rearrange("p j c -> p (j c)"),
                                           m == 0, m == MT - 1)
                    last.then_inc(a_mm, 1)
                    q += 1

            pe.wait_ge(const_set, 1)
            for m in range(MT):
                pe.wait_ge(b_lo, m + 1)
                for half in range(HALVES):
                    for i in (HI, LO):
                        last = pe.matmul(ps[:, half, :], ones[:], adj[:, i, m, half * BANK:(half + 1) * BANK],
                                         start=(m == 0 and i == HI), stop=(m == MT - 1 and i == LO))
            last.then_inc(b_mm, 1)

            def add_bias(dst, stat, mov):
                return pe.matmul(dst, stat, mov, start=False, stop=True)

            with pe.Fori(0, PAIRS) as it:
                for j in range(2):
                    lo0 = it * (2 * B_LO) + (B_PRE + j * B_LO)

                    def bank_free(r):
                        if j == 0:
                            if r == 0:
                                pe.wait_ge(gate_act, it * GATES + GATE_PRE)
                            if r == 4:
                                pe.wait_ge(fin_add, it * 4 + FIN_PRE)
                        else:
                            pe.wait_ge(b_lo, lo0 - B_LO + b_lo_of(r))
                    pe.wait_ge(b_lo, lo0 if j == 0 else lo0 - 2)
                    for half in range(HALVES):
                        bank_free(half)
                        adj_by(ps[:, half, :], lambda i, m: node[:, i, m * P:(m + 1) * P],
                               half).then_inc(b_mm, 1)
                    for u in range(2):
                        bank_free(2 + u)
                        pe.wait_ge(b_lo, lo0 + b_lo_of(u))
                        for t in range(4):
                            nt = (4 * u + t) * P
                            dst = ps[:, 2 + u, t * F:(t + 1) * F]
                            product(dst, lambda i: z[:, i, nt:nt + P], lambda i: wgs[:, i, 0, :], True, False)
                            last = add_bias(dst, rowsum[:, nt:nt + P], brow[:, 0, :])
                        last.then_inc(b_mm, 1)
                    for half in range(HALVES):
                        bank_free(4 + half)

                        def h_ready(m):
                            if m % 4 == 0:
                                pe.wait_ge(b_lo, lo0 + b_lo_of(2 + m // 4))
                        adj_by(ps[:, 4 + half, :], lambda i, m: node[:, i, m * P:(m + 1) * P], half,
                               h_ready if half == 0 else None).then_inc(b_mm, 1)
                    for half in range(HALVES):
                        bank_free(6 + half)
                        pe.wait_ge(b_lo, lo0 + b_lo_of(4 + half))
                        cols = slice(half * BANK, (half + 1) * BANK)
                        product(ps[:, 6 + half, :], lambda i: wgs[:, i, 1, :], lambda i: z[:, i, cols],
                                True, False)
                        add_bias(ps[:, 6 + half, :], brow[:, 1, :], rowsum[:, cols]).then_inc(b_mm, 1)

                gate0 = it * GATES + GATE_PRE
                for k in range(LUNITS):
                    p, s, first = STEPS[k // 2]
                    j = k % 2
                    _, n = windows(p)
                    cols = slice(first, first + p * (n - 1) + 1, p)
                    if k == 0:
                        pe.wait_ge(b_lo, it * (2 * B_LO) + (B_PRE + 2 * B_LO))
                    if k >= 2:
                        pe.wait_ge(gate_act, gate0 + GATE0[k - 1])
                    if k >= 2 and s == 0 and p > 1:
                        pe.wait_ge(h_done, it * LUNITS + (k - 1))
                    for g in gates_of(s):
                        last = product(ps[:, 4 * j + g, 0:n], lambda i: lw[:, i, p - 1, g * F:(g + 1) * F],
                                       lambda i: ht[:, i, j, cols], True, s == 0)
                        if s == 0:
                            last.then_inc(gate_mm, 1)
                    if s > 0:
                        pe.wait_ge(h_done, it * LUNITS + (k - 1))
                        for g in gates_of(s):
                            product(ps[:, 4 * j + g, 0:n], lambda i: lw[:, i, whh(p), g * F:(g + 1) * F],
                                    lambda i: hstep[:, i, j, 0:n], False, True).then_inc(gate_mm, 1)
                pe.wait_ge(gate_act, gate0 + GATES)
                for j in range(2):
                    pe.wait_ge(h_done, it * LUNITS + (LUNITS - 1 + j))
                    for u in range(2):
                        for t in range(4):
                            nt = (4 * u + t) * P
                            dst = ps[:, 4 + 2 * j + u, t * F:(t + 1) * F]
                            pe.matmul(dst, ht[:, HI, j, nt:nt + P], ident[:], start=True, stop=False)
                            last = pe.matmul(dst, ht[:, LO, j, nt:nt + P], ident[:], start=False, stop=True)
                        last.then_inc(fin_mm, 1)

        @block.scalar
        def _(act):
            def x_hi(batch, done):
                nc.scalar.activation(node[:, HI, :], xb[:, bass.ds(batch, 1)].rearrange("p b t c -> p (b t c)"),
                                     ACT.Copy).then_inc(done, 1)

            act.wait_ge(x0_in, 16)
            nc.scalar.activation(node[:, HI, :], xb[:, 0].rearrange("p t c -> p (t c)"),
                                 ACT.Copy).then_inc(a_hi, 1)
            for m in range(MT):
                act.wait_ge(sq_done, m + 1)
                nc.scalar.activation(adj[:, HI, m, :], square[:, m, :], ACT.Copy).then_inc(a_hi, 1)
            act.wait_ge(w0_in, 48)
            nc.scalar.activation(w1s[:, HI, :], w0_raw[:, 0:H1], ACT.Copy)
            nc.scalar.activation(w2s[:, HI, :, :].rearrange("p k g -> p (k g)"), w0_raw[:, H1:H1 + K2 * H2],
                                 ACT.Copy)
            nc.scalar.activation(w3s[:, :, HI, :], w0_raw[:, H1 + K2 * H2:].rearrange("p (k g) -> p k g", k=K3),
                                 ACT.Copy).then_inc(a_hi, 1)
            act.wait_ge(xr_in, 16 * (B - 1))

            with act.Fori(0, PAIRS) as it:
                for j in range(2):
                    mm0 = it * A_MM_PAIR + j * A_MM
                    q = 0

                    def hi_part(dst, func):
                        act.wait_ge(a_mm, mm0 + (q + 1))
                        nc.scalar.activation(dst, ps[:, (j * A_MM + q) % BANKS, :], func).then_inc(a_hi, 1)

                    for half in range(HALVES):
                        hi_part(y1[:, HI, half * BANK:(half + 1) * BANK], ACT.Copy)
                        q += 1
                    for u in range(P1):
                        hi_part(h1[:, HI, 2 * u:2 * u + 2, :].rearrange("p t g -> p (t g)"), ACT.Relu)
                        q += 1
                    for half in range(HALVES):
                        for k in range(K2):
                            hi_part(y2[:, HI, k, half * BANK:(half + 1) * BANK], ACT.Copy)
                            q += 1
                    x_hi((it * 2 + (j + 1)) % B, a_hi)
                    for half in range(HALVES):
                        for g in range(K3):
                            hi_part(h2[:, HI, g, half * BANK:(half + 1) * BANK], ACT.Relu)
                            q += 1
                    for u in range(P3):
                        act.wait_ge(a_mm, mm0 + (q + 1))
                        if u >= 2:
                            act.wait_ge(a_lo, it * A_LO_PAIR + (A_PRE + a_lo_of(j * A_MM + q - 2)))
                        nc.scalar.activation(
                            cross[:, u % 2], ps[:, (j * A_MM + q) % BANKS, :].rearrange(
                                "p (t a c) -> p t a c", t=2, a=2)[:, :, 1, :], ACT.Copy).then_inc(a_hi, 1)
                        q += 1

            act.wait_ge(a_mm, PAIRS * A_MM_PAIR)
            for m in range(MT):
                act.wait_ge(adj_in[m], 32)
                nc.scalar.activation(adj[:, HI, m, :], adj_raw[:, m, :], ACT.Copy).then_inc(b_hi, 1)
            act.wait_ge(b_mm, 1)
            nc.scalar.activation(ht[:, HI, 0, 0:N], ps[:, 0:2, :].rearrange("p a c -> p (a c)"),
                                 ACT.Copy).then_inc(b_hi, 1)
            act.wait_ge(lw_in, 16 * 8)
            act.wait_ge(const_set, 1)
            nc.scalar.activation(warm[:], lb[:, 0:1], ACT.Sigmoid).then_inc(gate_act, 1)
            act.wait_ge(b_lo, MT)
            for k in range(LW):
                nc.scalar.activation(lw[:, HI, k, :], lw_raw[:, k, :], ACT.Copy).then_inc(b_hi, 1)

            with act.Fori(0, PAIRS) as it:
                for j in range(2):
                    mm0 = it * (2 * B_MM) + (1 + j * B_MM)

                    def hi_part(r, dst, func):
                        act.wait_ge(b_mm, mm0 + (r + 1))
                        nc.scalar.activation(dst, ps[:, r, :], func).then_inc(b_hi, 1)

                    for r in range(2):
                        hi_part(r, z[:, HI, r * BANK:(r + 1) * BANK], ACT.Copy)
                    for r in range(2):
                        hi_part(2 + r, node[:, HI, r * BANK:(r + 1) * BANK], ACT.Relu)
                    for r in range(2):
                        hi_part(4 + r, z[:, HI, r * BANK:(r + 1) * BANK], ACT.Copy)
                    x_hi((it * 2 + (j + 1)) % B, b_hi)
                    for r in range(2):
                        hi_part(6 + r, ht[:, HI, j, r * BANK:(r + 1) * BANK], ACT.Relu)

                for k in range(LUNITS):
                    p, s, _ = STEPS[k // 2]
                    j = k % 2
                    _, n = windows(p)
                    if k >= 2:
                        act.wait_ge(h_done, it * LUNITS + (k - 1))
                    for a, g in enumerate(gates_of(s)):
                        act.wait_ge(gate_mm, it * GATES + (GATE0[k] + a + 1))
                        col = (p - 1) * 4 + g
                        nc.scalar.activation(gates[:, j, g, 0:n], ps[:, 4 * j + g, 0:n],
                                             ACT.Tanh if g == GG else ACT.Sigmoid,
                                             bias=lb[:, col:col + 1]).then_inc(gate_act, 1)
                    act.wait_ge(cell_done, it * LUNITS + (k + 1))
                    nc.scalar.activation(gates[:, j, GG, 0:n], gates[:, j, 4, 0:n],
                                         ACT.Tanh).then_inc(tanh_done, 1)

        @block.vector
        def _(dve):

            def lo_part(dst, src, hi, done):
                nc.vector.tensor_tensor(dst, src, f32(hi), ALU.subtract).then_inc(done, 1)

            def lo_relu(dst, src, hi, done):
                nc.vector.scalar_tensor_tensor(out=dst, in0=src, scalar=0.0, in1=f32(hi), op0=ALU.max,
                                               op1=ALU.subtract).then_inc(done, 1)

            def x_lo(batch, done):
                lo_part(node[:, LO, :], xb[:, bass.ds(batch, 1)].rearrange("p b t c -> p (b t c)"),
                        node[:, HI, :], done)

            def group_stats(groups, own_at):
                nc.vector.memset(took_wait[:], 0.0)
                for g, rows in groups:
                    last = nc.vector.bn_stats(stats[:, g, :], rows)
                last.then_inc(own, 1)
                dve.wait_ge(own, own_at + 1)
                nc.vector.memset(took_wait[:], 0.0)
                for g, _ in groups:
                    last = nc.vector.bn_aggr(mv[:, g, :], stats[:, g, :])
                last.then_inc(own, 1)

            def normalise(groups, own_at, done):
                g0, g1 = groups[0][0], groups[-1][0] + 1
                v, y, t = (newton[:, i, g0:g1] for i in range(3))
                as_int = lambda ap: ap.bitcast(I32)
                dve.wait_ge(own, own_at)
                nc.vector.tensor_scalar(v, mv[:, g0:g1, 1], EPS, None, ALU.add).then_inc(own, 1)
                dve.wait_ge(own, own_at + 1)
                nc.vector.tensor_scalar(as_int(t), as_int(v), 1, None,
                                        ALU.logical_shift_right).then_inc(own, 1)
                dve.wait_ge(own, own_at + 2)
                nc.vector.tensor_scalar(as_int(y), as_int(t), -1.0, float(0x5F3759DF), ALU.mult,
                                        ALU.add).then_inc(own, 1)
                for i in range(NEWTON):
                    dve.wait_ge(own, own_at + (3 + 3 * i))
                    nc.vector.scalar_tensor_tensor(out=t, in0=y, scalar=-0.5, in1=v, op0=ALU.mult,
                                                   op1=ALU.mult).then_inc(own, 1)
                    dve.wait_ge(own, own_at + (3 + 3 * i + 1))
                    nc.vector.tensor_tensor(t, t, y, ALU.mult).then_inc(own, 1)
                    dve.wait_ge(own, own_at + (3 + 3 * i + 2))
                    nc.vector.scalar_tensor_tensor(out=y, in0=t, scalar=1.5, in1=y, op0=ALU.add,
                                                   op1=ALU.mult).then_inc(own, 1)
                dve.wait_ge(own, own_at + RSQRT_OWN)
                for g, rows in groups:
                    last = nc.vector.tensor_scalar(rows, rows, mv[:, g, 0:1], newton[:, 1, g:g + 1],
                                                   ALU.subtract, ALU.mult)
                last.then_inc(done, 1)

            dve.wait_ge(a_hi, 1)
            lo_part(node[:, LO, :], xb[:, 0].rearrange("p t c -> p (t c)"), node[:, HI, :], a_lo)

            def square_tile(m):
                dve.wait_ge(adj_in[m], 16)
                nc.vector.tensor_tensor(square[:, m, :], square[:, m, :], square[:, m, :],
                                        ALU.mult).then_inc(sq_done, 1)

            square_tile(0)
            for m in range(MT):
                if m + 1 < MT:
                    square_tile(m + 1)
                dve.wait_ge(a_hi, 1 + (m + 1))
                lo_part(adj[:, LO, m, :], square[:, m, :], adj[:, HI, m, :], a_lo)
            dve.wait_ge(a_hi, A_PRE)
            nc.vector.tensor_tensor(w1s[:, LO, :], w0_raw[:, 0:H1], f32(w1s[:, HI, :]), ALU.subtract)
            nc.vector.tensor_tensor(w2s[:, LO, :, :].rearrange("p k g -> p (k g)"), w0_raw[:, H1:H1 + K2 * H2],
                                    f32(w2s[:, HI, :, :]).rearrange("p k g -> p (k g)"), ALU.subtract)
            lo_part(w3s[:, :, LO, :], w0_raw[:, H1 + K2 * H2:].rearrange("p (k g) -> p k g", k=K3),
                    w3s[:, :, HI, :], a_lo)

            nc.vector.memset(sel[:], 0.0).then_inc(own, 1)
            dve.wait_ge(own, 1)
            for row, col in ((0, 0), (32, 0), (64, 1), (0, 2), (64, 2), (32, 3)):
                nc.vector.memset(sel[row:row + 1, col:col + 1], 1.0)
            dve.wait_ge(lw_in, 16 * 8)
            nc.vector.tensor_tensor(lb[:], lb_raw[:, 0, :], lb_raw[:, 1, :], ALU.add)
            nc.vector.tensor_copy(wgs[:, HI, :, :], wg_raw[:, 0:2, :])
            nc.vector.tensor_copy(bparts[:, HI, :, :], wg_raw[:, 2:4, :]).then_inc(own, 1)
            dve.wait_ge(own, 2)
            nc.vector.tensor_tensor(wgs[:, LO, :, :], wg_raw[:, 0:2, :], f32(wgs[:, HI, :, :]), ALU.subtract)
            nc.vector.tensor_tensor(bparts[:, LO, :, :], wg_raw[:, 2:4, :], f32(bparts[:, HI, :, :]),
                                    ALU.subtract)
            nc.vector.tensor_scalar(brow[:], f32(bparts[:, HI, :, :]), sel[:, 2:3], None,
                                    ALU.mult).then_inc(own, 1)
            dve.wait_ge(own, 3)
            nc.vector.scalar_tensor_tensor(out=brow[:].rearrange("p a c -> p (a c)"),
                                           in0=f32(bparts[:, LO, :, :]).rearrange("p a c -> p (a c)"),
                                           scalar=sel[:, 3:4], in1=f32(brow[:]).rearrange("p a c -> p (a c)"),
                                           op0=ALU.mult, op1=ALU.add)
            dve.wait_ge(eye_set, 2)
            nc.vector.tensor_copy(ident[:], ident_f[:]).then_inc(own, 1)
            dve.wait_ge(own, 4)
            nc.vector.memset(ident_f[:], 1.0).then_inc(own, 1)
            dve.wait_ge(own, 5)
            nc.vector.tensor_copy(ones[:], ident_f[:]).then_inc(const_set, 1)
            own_pre = 5

            A_OWN = 2 * (2 * P3) + 2 * A3 + RSQRT_OWN
            with dve.Fori(0, PAIRS) as it:
                own0 = it * A_OWN + own_pre
                for j in range(2):
                    hi0 = it * A_HI_PAIR + (A_PRE + j * A_LO)
                    q = 0
                    n_hi = 0

                    def bank():
                        return ps[:, (j * A_MM + q) % BANKS, :]

                    def hi_ready():
                        dve.wait_ge(a_hi, hi0 + (n_hi + 1))

                    for half in range(HALVES):
                        hi_ready()
                        cols = slice(half * BANK, (half + 1) * BANK)
                        lo_part(y1[:, LO, cols], bank(), y1[:, HI, cols], a_lo)
                        q, n_hi = q + 1, n_hi + 1
                    for u in range(P1):
                        hi_ready()
                        lo_relu(h1[:, LO, 2 * u:2 * u + 2, :].rearrange("p t g -> p (t g)"), bank(),
                                h1[:, HI, 2 * u:2 * u + 2, :].rearrange("p t g -> p (t g)"), a_lo)
                        q, n_hi = q + 1, n_hi + 1
                    for half in range(HALVES):
                        for k in range(K2):
                            hi_ready()
                            cols = slice(half * BANK, (half + 1) * BANK)
                            lo_part(y2[:, LO, k, cols], bank(), y2[:, HI, k, cols], a_lo)
                            q, n_hi = q + 1, n_hi + 1
                    hi_ready()
                    x_lo((it * 2 + (j + 1)) % B, a_lo)
                    n_hi += 1
                    for half in range(HALVES):
                        for g in range(K3):
                            hi_ready()
                            cols = slice(half * BANK, (half + 1) * BANK)
                            lo_relu(h2[:, LO, g, cols], bank(), h2[:, HI, g, cols], a_lo)
                            q, n_hi = q + 1, n_hi + 1
                    for u in range(P3):
                        own_at = own0 + (j * 2 * P3 + 2 * u)
                        hi_ready()
                        if u > 0:
                            dve.wait_ge(a_lo, it * A_LO_PAIR + (A_PRE + a_lo_of(j * A_MM + q - 1)))
                        nc.vector.tensor_tensor(
                            s3full[:], bank().rearrange("p (t a c) -> p t a c", t=2, a=2)[:, :, 0, :],
                            cross[:, u % 2], ALU.add).then_inc(own, 1)
                        dve.wait_ge(own, own_at + 1)
                        nc.vector.tensor_copy(s3[:, HI, 2 * u:2 * u + 2, j, :], s3full[:]).then_inc(own, 1)
                        dve.wait_ge(own, own_at + 2)
                        lo_part(s3[:, LO, 2 * u:2 * u + 2, j, :], s3full[:],
                                s3[:, HI, 2 * u:2 * u + 2, j, :], a_lo)
                        q, n_hi = q + 1, n_hi + 1
                every = []
                for u in range(A3):
                    own_at = own0 + (4 * P3 + 2 * u)
                    q = 2 * A_MM + u
                    dve.wait_ge(a_mm, it * A_MM_PAIR + (q + 1))
                    rows = xb[:, bass.ds(it * 2, 2), 2 * u:2 * u + 2, :]
                    nc.vector.tensor_tensor(rows, rows, ps[:, q % BANKS, :].rearrange(
                        "p (t j c) -> p j t c", t=2, j=2), ALU.add).then_inc(a_lo, 1)
                    dve.wait_ge(a_lo, it * A_LO_PAIR + (A_PRE + 2 * A_LO + u + 1))
                    groups = [(8 * j + 2 * u + t,
                               xb[:, bass.ds(it * 2 + j, 1), 2 * u + t, :].rearrange("p b c -> p (b c)"))
                              for j in range(2) for t in range(2)]
                    group_stats(groups, own_at)
                    every += groups
                every.sort(key=lambda group: group[0])
                normalise(every, own0 + (4 * P3 + 2 * A3), a_ln)
            own_pre += PAIRS * A_OWN

            for m in range(MT):
                dve.wait_ge(b_hi, m + 1)
                lo_part(adj[:, LO, m, :], adj_raw[:, m, :], adj[:, HI, m, :], b_lo)
            dve.wait_ge(b_hi, MT + 1)
            nc.vector.tensor_tensor(ht[:, LO, 0, 0:N], ps[:, 0:2, :].rearrange("p a c -> p (a c)"),
                                    f32(ht[:, HI, 0, 0:N]), ALU.subtract)
            nc.vector.tensor_scalar(rowsum[:], f32(ht[:, HI, 0, 0:N]), sel[:, 0:1], None,
                                    ALU.mult).then_inc(own, 1)
            dve.wait_ge(own, own_pre + 1)
            nc.vector.scalar_tensor_tensor(out=rowsum[:], in0=f32(ht[:, LO, 0, 0:N]), scalar=sel[:, 1:2],
                                           in1=f32(rowsum[:]), op0=ALU.mult, op1=ALU.add).then_inc(b_lo, 1)
            dve.wait_ge(b_lo, MT + 1)
            for i in (HI, LO):
                last = nc.vector.memset(f32(ht[:, i, :, N:HTW]), 0.0)
            last.then_inc(fin_add, 1)
            for k in range(LW):
                dve.wait_ge(b_hi, MT + 1 + (k + 1))
                lo_part(lw[:, LO, k, :], lw_raw[:, k, :], lw[:, HI, k, :], b_lo)
            own_pre += 1

            def lstm_own(k):
                return sum(2 if STEPS[i // 2][1] == 0 else 4 for i in range(k))

            FIN_OWN = 2 * 2 + RSQRT_OWN
            B_OWN = lstm_own(LUNITS) + 2 * FIN_OWN
            with dve.Fori(0, PAIRS) as it:
                for j in range(2):
                    hi0 = it * (2 * B_LO) + (B_PRE + j * B_LO)

                    def cols(r):
                        return slice((r % 2) * BANK, (r % 2 + 1) * BANK)

                    for r in range(2):
                        dve.wait_ge(b_hi, hi0 + (r + 1))
                        lo_part(z[:, LO, cols(r)], ps[:, r, :], z[:, HI, cols(r)], b_lo)
                    for r in range(2, 4):
                        dve.wait_ge(b_hi, hi0 + (r + 1))
                        lo_relu(node[:, LO, cols(r)], ps[:, r, :], node[:, HI, cols(r)], b_lo)
                    for r in range(4, 6):
                        dve.wait_ge(b_hi, hi0 + (r + 1))
                        lo_part(z[:, LO, cols(r)], ps[:, r, :], z[:, HI, cols(r)], b_lo)
                    dve.wait_ge(b_hi, hi0 + 7)
                    x_lo((it * 2 + (j + 1)) % B, b_lo)
                    for r in range(6, 8):
                        dve.wait_ge(b_hi, hi0 + (r + 2))
                        lo_relu(ht[:, LO, j, cols(r)], ps[:, r, :], ht[:, HI, j, cols(r)], b_lo)

                own0 = it * B_OWN + own_pre
                for k in range(LUNITS):
                    p, s, first = STEPS[k // 2]
                    j = k % 2
                    nw, n = windows(p)
                    gate = lambda g: gates[:, j, g, 0:n]
                    own_at = own0 + lstm_own(k)
                    act_at = it * GATES + (GATE_PRE + GATE0[k])
                    dve.wait_ge(gate_act, act_at + 2)
                    if s == 0:
                        nc.vector.tensor_tensor(gate(4), gate(GI), gate(GG), ALU.mult).then_inc(cell_done, 1)
                        used = 0
                    else:
                        nc.vector.tensor_tensor(gate(GI), gate(GI), gate(GG), ALU.mult).then_inc(own, 1)
                        dve.wait_ge(gate_act, act_at + 3)
                        nc.vector.tensor_tensor(gate(GF), gate(GF), gate(4), ALU.mult).then_inc(own, 1)
                        dve.wait_ge(own, own_at + 2)
                        nc.vector.tensor_tensor(gate(4), gate(GI), gate(GF), ALU.add).then_inc(cell_done, 1)
                        used = 2
                    if s == p - 1:
                        n, at = nw, slice(first, first + p * (nw - 1) + 1, p)
                        dst = [ht[:, i, j, at] for i in (HI, LO)]
                    else:
                        dst = [hstep[:, i, j, 0:n] for i in (HI, LO)]
                    dve.wait_ge(tanh_done, it * LUNITS + (k + 1))
                    h = gates[:, j, GO, 0:n]
                    nc.vector.tensor_tensor(h, h, gates[:, j, GG, 0:n], ALU.mult).then_inc(own, 1)
                    dve.wait_ge(own, own_at + (used + 1))
                    nc.vector.tensor_copy(dst[HI], h).then_inc(own, 1)
                    dve.wait_ge(own, own_at + (used + 2))
                    lo_part(dst[LO], h, dst[HI], h_done)

                for j in range(2):
                    own_at = own0 + (lstm_own(LUNITS) + j * FIN_OWN)
                    every = []
                    for u in range(2):
                        dve.wait_ge(fin_mm, it * 4 + (2 * j + u + 1))
                        rows = xb[:, bass.ds(it * 2 + j, 1), 4 * u:4 * u + 4, :].rearrange(
                            "p b t c -> p (b t c)")
                        nc.vector.tensor_tensor(rows, rows, ps[:, 4 + 2 * j + u, :],
                                                ALU.add).then_inc(fin_add, 1)
                        dve.wait_ge(fin_add, it * 4 + (FIN_PRE + 2 * j + u + 1))
                        groups = [(8 * j + 4 * u + t,
                                   xb[:, bass.ds(it * 2 + j, 1), 4 * u + t, :].rearrange("p b c -> p (b c)"))
                                  for t in range(4)]
                        group_stats(groups, own_at + 2 * u)
                        every += groups
                    normalise(every, own_at + 4, out_ready)


def kernel(x, adj, L0_gnn_W1, L0_gnn_W2, L0_gnn_W3, L1_gnn_Wg0, L1_gnn_bg0, L1_gnn_Wg1, L1_gnn_bg1,
           L1_gnn_Wih, L1_gnn_Whh, L1_gnn_bih, L1_gnn_bhh):
    import concourse.bacc as bacc
    from concourse.bass_utils import run_bass_kernel_spmd

    def rows(b):
        return np.broadcast_to(b, (P, b.shape[0]))

    def per_feature(b):
        return np.asarray(b).reshape(SKIPS, 4, P).transpose(2, 0, 1).reshape(P, SKIPS * 4)

    host = {
        "x": x, "adj_t": np.asarray(adj).T, "w1": L0_gnn_W1, "w2": L0_gnn_W2, "w3": L0_gnn_W3,
        "wg0": L1_gnn_Wg0, "bg0": rows(np.asarray(L1_gnn_bg0)), "wg1": L1_gnn_Wg1,
        "bg1": rows(np.asarray(L1_gnn_bg1)), "wih_t": np.asarray(L1_gnn_Wih).transpose(0, 2, 1),
        "whh_t": np.asarray(L1_gnn_Whh).transpose(0, 2, 1), "bih": per_feature(L1_gnn_bih),
        "bhh": per_feature(L1_gnn_bhh),
    }
    nc = bacc.Bacc("TRN2", target_bir_lowering=False, num_devices=1)
    arrays, args = {}, []
    for name, a in host.items():
        a = np.ascontiguousarray(a)
        arrays[f"in_{name}"] = a
        args.append(nc.dram_tensor(f"in_{name}", a.shape, mybir.dt.from_np(a.dtype), kind="ExternalInput").ap())
    out = nc.dram_tensor("out_0", tuple(np.shape(x)), F32, kind="ExternalOutput").ap()
    build(nc, *args, out)
    r = run_bass_kernel_spmd(nc, [arrays], core_ids=[0])
    return r.results[0]["out_0"]
```

```python
from collections import namedtuple
from contextlib import ExitStack

import numpy as np

import concourse.bass as bass
import concourse.mybir as mybir

F32 = mybir.dt.float32
F32R = mybir.dt.float32r
I32 = mybir.dt.int32
ALU = mybir.AluOpType
ACT = mybir.ActivationFunctionType

P = 128
BANK = 512
BANKS = 8
HI, LO = 0, 1
EPS = 1e-5
NEWTON = 3
LN_STEPS = 2 + 3 + 3 * NEWTON
SKIPS = 4
GI, GF, GG, GO = range(4)


def build(nc, x, adj_t, w1, w2, w3, wg0, bg0, wg1, bg1, wih_t, whh_t, bih, bhh, out):
    B, N, F = x.shape
    H1, H2 = w1.shape[1], w2.shape[1]
    MT = N // P
    HALVES = N // BANK
    K2, K3 = H1 // P, H2 // P
    PAIRS = B // 2
    G4 = SKIPS * P
    assert F == P and HALVES == 2 and w3.shape[1] == F and wih_t.shape == (SKIPS, F, 4 * F)

    ctx = ExitStack()
    with ctx:
        base = (nc.sbuf_base + 63) // 64 * 64
        top = [base]

        def place(nbytes):
            at = top[0]
            top[0] += (nbytes + 63) // 64 * 64
            return at

        def sb(name, shape, dt, at=None):
            size = 4 * int(np.prod(shape[1:]))
            return nc.alloc_sbuf_tensor_at(name, shape, dt, offset=place(size) if at is None else at)

        KB = 1024
        adj_at = place(2 * MT * N * 4)
        adj = sb("adj", [P, 2, MT, N], F32R, adj_at)
        square = sb("square", [P, MT, N], F32, adj_at + MT * N * 4)
        xb = sb("xb", [P, B, MT, F], F32)
        node = sb("node", [P, 2, N], F32R)
        big_at = place(32 * KB)
        y1 = sb("y1", [P, 2, N], F32R, big_at)
        h1 = sb("h1", [P, 2, MT, H1], F32R, big_at + 8 * KB)
        h2 = sb("h2", [P, 2, K3, N], F32R, big_at)
        adj_raw = sb("adj_raw", [P, MT, N], F32, big_at)
        lw = sb("lw", [P, 2, 2 * SKIPS - 1, G4], F32R, big_at)
        rowsum = sb("rowsum", [P, N], F32R, big_at + 28 * KB)
        r2_at = place(16 * KB)
        y2 = sb("y2", [P, 2, K2, N], F32R, r2_at)
        w0_raw = sb("w0_raw", [P, H1 + K2 * H2 + K3 * F], F32, r2_at)
        z = sb("z", [P, 2, N], F32R, r2_at)
        hs_at = r2_at + 8 * KB
        HTW = N + 2
        h0 = sb("h0", [P, 2, N], F32R, hs_at)
        r3_at = place(16 * KB)
        s3 = sb("s3", [P, 2, MT, 2, F], F32R, r3_at)
        w0_at = place(4 * 2 * (H1 + K2 * H2 + K3 * F))
        w1s = sb("w1s", [P, 2, H1], F32R, w0_at)
        w2s = sb("w2s", [P, 2, K2, H2], F32R, w0_at + 8 * H1)
        w3s = sb("w3s", [P, K3, 2, F], F32R, w0_at + 8 * (H1 + K2 * H2))
        lw_raw_at = place(4 * (2 * SKIPS - 1) * G4 + 64)
        lw_raw = sb("lw_raw", [P, 2 * SKIPS - 1, G4], F32, lw_raw_at)
        ht = sb("ht", [P, 2, 2, HTW], F32R, r3_at)
        gates_at = (r3_at + 4 * 4 * HTW + 63) // 64 * 64
        gates = sb("gates", [P, 2, 5, BANK], F32, gates_at)
        hstep = sb("hstep", [P, 2, 2, BANK], F32R, gates_at + 4 * 10 * BANK)
        assert gates_at + 4 * 14 * BANK <= lw_raw_at + 4 * (2 * SKIPS - 1) * G4 + 64
        wg_raw = sb("wg_raw", [P, 4, F], F32)
        wgs = sb("wgs", [P, 2, 2, F], F32R)
        cross_at = place(2 * KB)
        cross = sb("cross", [P, 2, 2, F], F32, cross_at)
        bparts = sb("bparts", [P, 2, 2, F], F32R, cross_at)
        brow = sb("brow", [P, 2, F], F32R)
        ident_f = sb("ident_f", [P, P], F32)
        ident = sb("ident", [P, P], F32R)
        ones = sb("ones", [P, P], F32R)
        lb_raw = sb("lb_raw", [P, 2, SKIPS * 4], F32)
        lb = sb("lb", [P, SKIPS * 4], F32)
        sel = sb("sel", [P, 4], F32)
        s3full = sb("s3full", [P, 2, F], F32)
        stats = sb("stats", [P, 16, 6], F32)
        mv = sb("mv", [P, 16, 2], F32)
        took_wait = sb("took_wait", [P, 2], F32)
        newton = sb("newton", [P, 3, 16], F32)
        assert top[0] <= nc.sbuf_usable_end

        ps = ctx.enter_context(nc.psum_tensor("ps", [P, BANKS, BANK], F32))

        def sem(name):
            return ctx.enter_context(nc.semaphore(name))

        x0_in = sem("x0_in")
        xr_in = sem("xr_in")
        adj_in = [sem(f"adj_in{m}") for m in range(MT)]
        w1_in = sem("w1_in")
        w0_in = sem("w0_in")
        lw_in = sem("lw_in")
        eye_set = sem("eye_set")
        const_set = sem("const_set")
        own = sem("own")
        ln_step = sem("ln_step")
        cell_step = sem("cell_step")
        sq_done = sem("sq_done")
        sq_act = sem("sq_act")
        adj_used = sem("adj_used")
        a_mm, a_hi, a_lo = sem("a_mm"), sem("a_hi"), sem("a_lo")
        a_ln = sem("a_ln")
        b_mm, b_hi, b_lo = sem("b_mm"), sem("b_hi"), sem("b_lo")
        lw_hi, lw_lo = sem("lw_hi"), sem("lw_lo")
        gate_mm = sem("gate_mm")
        gate_act = sem("gate_act")
        cell_done = sem("cell_done")
        tanh_done = sem("tanh_done")
        h_done = sem("h_done")
        fin_mm = sem("fin_mm")
        fin_add = sem("fin_add")
        out_ready = sem("out_ready")
        out_done = sem("out_done")

        A1, P1, A2, P2, P3, A3 = HALVES, MT * H1 // BANK, HALVES * K2, HALVES * K3, MT // 2, MT // 2
        A_MM = A1 + P1 + A2 + P2 + P3
        A_LO = A_MM + 1
        A_MM_PAIR, A_LO_PAIR = 2 * A_MM + A3, 2 * A_LO + A3
        A_HI_PAIR = 2 * A_LO
        A_PRE = 1 + MT + 2
        W1_AT = 5
        assert A_MM_PAIR % BANKS == 0

        def a_lo_of(q):
            if q < 0:
                return a_lo_of(q + A_MM_PAIR) - A_LO_PAIR
            if q >= 2 * A_MM:
                return 2 * A_LO + (q - 2 * A_MM) + 1
            j, r = divmod(q, A_MM)
            return j * A_LO + r + 1 + (r >= A1 + P1 + A2)

        LW = 2 * SKIPS - 1
        B_PRE = MT + 1
        B_MM, B_LO = 8, 9
        GB = 6

        def b_lo_of(r):
            return r + 1 + (r >= 6)

        Step = namedtuple("Step", "stream p s w0 nw n back")
        X, Y = 0, 1

        def step(stream, p, s, w0=0, back=None):
            nw = min(N // p, BANK)
            return Step(stream, p, s, w0, nw, nw + nw % 2, (2 if stream == X else 1) if back is None else back)

        SLOT = [("adj_x", 0), step(X, 3, 0), step(Y, 1, 0), step(X, 3, 1), step(Y, 1, 0, BANK),
                ("adj_x", 1), step(X, 3, 2), ("wg0", 0), ("wg0", 1), step(Y, 2, 0), step(X, 4, 0),
                ("adj_h", 0, 0, MT), step(X, 4, 1), ("adj_h", 1, 0, MT // 2), step(X, 4, 2),
                ("adj_h", 1, MT // 2, MT), ("split",), step(X, 4, 3), ("wg1", 0), ("wg1", 1),
                ("ahead",), ("fin", 0, 2), ("fin", 1, 2), ("stats", 2), step(Y, 2, 1), ("norm", 2)]
        LAST = [step(Y, 1, 0), step(X, 3, 0), step(Y, 1, 0, BANK), step(X, 3, 1), step(Y, 2, 0),
                step(X, 3, 2), step(Y, 2, 1), step(X, 4, 0), step(Y, 3, 0), step(X, 4, 1),
                step(Y, 3, 1), step(X, 4, 2), step(Y, 3, 2), step(X, 4, 3), step(Y, 4, 0),
                ("fin", 0, 2), ("fin", 1, 2), step(Y, 4, 1), ("stats", 2), step(Y, 4, 2), ("norm", 2),
                step(Y, 4, 3), ("fin", 0, 1), ("fin", 1, 1), ("stats", 1), ("norm", 1)]
        SLOTS = B + 1

        def items(slot):
            if slot == SLOTS - 1:
                return LAST
            conv, y, x_ = True, slot >= 1, slot >= 2
            kept = []
            for item in SLOT:
                if isinstance(item, Step):
                    keep = y if item.stream == Y else x_
                else:
                    keep = {"fin": x_, "stats": x_, "norm": x_, "ahead": x_ and y}.get(item[0], conv)
                if keep:
                    kept.append(item)
                if slot == 0 and item == ("wg0", 1):
                    kept.append(("weights",))
                if slot == 0 and item == ("wg1", 1):
                    kept.append(("pair_stats",))
                if slot == 1 and item == step(Y, 2, 0):
                    kept.append(("pair_scale",))
            return kept

        def gates_of(s):
            return (GI, GG, GO) if s == 0 else (GI, GG, GF, GO)

        def steps_of(slot):
            return [item for item in items(slot) if isinstance(item, Step)]

        def count(slot, name):
            return sum(item[0] == name for item in items(slot) if not isinstance(item, Step))

        CELL_STEPS = (2, 4)
        PER_SLOT = {
            "mm": lambda n: B_MM * (n < B),
            "lo": lambda n: B_LO * (n < B),
            "gate": lambda n: sum(len(gates_of(u.s)) for u in steps_of(n)),
            "unit": lambda n: len(steps_of(n)),
            "cell": lambda n: sum(CELL_STEPS[u.s > 0] for u in steps_of(n)),
            "fin": lambda n: count(n, "fin"),
            "norm": lambda n: count(n, "norm") * LN_STEPS,
        }
        AHEAD = {k: [sum(f(m) for m in range(n)) for n in range(SLOTS + 1)] for k, f in PER_SLOT.items()}
        LOOP0 = 2
        TURNS = (B - LOOP0) // 2
        PER_TURN = {k: v[LOOP0 + 2] - v[LOOP0] for k, v in AHEAD.items()}
        assert PER_TURN["gate"] % GB == 0
        FIN_PRE = 1

        def ahead(what, slot, turn, more=0):
            n = AHEAD[what][slot] + more
            return n if turn is None else turn * PER_TURN[what] + n

        def batch_of(slot, turn, back):
            n = slot - back
            return n if turn is None else turn * 2 + n

        def slots(eng, body):
            for slot in range(LOOP0):
                body(slot, None)
            with eng.Fori(0, TURNS) as turn:
                for slot in (LOOP0, LOOP0 + 1):
                    body(slot, turn)
            for slot in range(B, SLOTS):
                body(slot, None)

        def before(slot, k, same):
            back, at = 0, k
            while True:
                own_steps = steps_of(slot - back)
                for i in range(at - 1, -1, -1):
                    if same(own_steps[i], back):
                        return sum(len(steps_of(slot - b)) for b in range(1, back + 1)) + k - i
                back += 1
                if slot - back < 1:
                    return None
                at = len(steps_of(slot - back))

        def needs(slot, k):
            u = steps_of(slot)[k]
            if u.s > 0:
                return before(slot, k, lambda v, b: b + v.back == u.back and (v.p, v.s) == (u.p, u.s - 1))
            if u.p == 1:
                return None
            return before(slot, k, lambda v, b: b + v.back == u.back and (v.p, v.s) == (u.p - 1, u.p - 2))

        def place_before(slot, k):
            u = steps_of(slot)[k]
            return before(slot, k, lambda v, b: v.stream == u.stream)

        def columns(u, nw):
            first = u.w0 * u.p + u.s
            return slice(first, first + u.p * (nw - 1) + 1, u.p)

        def loop_slot_steps_match():
            for slot in (LOOP0, LOOP0 + 1):
                for k in range(len(steps_of(slot))):
                    assert needs(slot, k) == needs(slot + 2, k)

        loop_slot_steps_match()

        def whh(p):
            return SKIPS + p - 2

        def f32(ap):
            return ap.bitcast(F32)

        block = ctx.enter_context(nc.Block())

        @block.sync
        def _(sp):
            for m in range(MT):
                if m == 1:
                    sp.dma_start(xb[:, 0], x[0].rearrange("(t p) c -> p t c", p=P)).then_inc(x0_in, 16)
                if m == W1_AT:
                    sp.dma_start(w0_raw[:, 0:H1], w1).then_inc(w1_in, 16)
                sp.dma_start(square[:, m, :], adj_t[m * P:(m + 1) * P, :]).then_inc(adj_in[m], 16)
            sp.dma_start(w0_raw[:, H1:H1 + K2 * H2].rearrange("p (k g) -> p k g", k=K2),
                         w2.rearrange("(k p) g -> p k g", p=P)).then_inc(w0_in, 16)
            sp.dma_start(w0_raw[:, H1 + K2 * H2:].rearrange("p (k g) -> p k g", k=K3),
                         w3.rearrange("(k p) g -> p k g", p=P)).then_inc(w0_in, 16)
            for b in range(1, B):
                sp.dma_start(xb[:, b], x[b].rearrange("(t p) c -> p t c", p=P)).then_inc(xr_in, 16)
            for k, small in enumerate((wg0, wg1, bg0, bg1)):
                sp.dma_start(wg_raw[:, k, :], small).then_inc(lw_in, 16)
            sp.dma_start(lb_raw[:, 0, :], bih).then_inc(lw_in, 16)
            sp.dma_start(lb_raw[:, 1, :], bhh).then_inc(lw_in, 16)
            sp.dma_start(lw_raw[:, 0:SKIPS, :], wih_t.rearrange("s f g -> f s g")).then_inc(lw_in, 16)
            sp.dma_start(lw_raw[:, SKIPS:, :], whh_t[1:].rearrange("s f g -> f s g")).then_inc(lw_in, 16)
            sp.wait_ge(a_mm, PAIRS * A_MM_PAIR - A3)
            for m in range(MT):
                sp.dma_start(adj_raw[:, m, :], adj_t[m * P:(m + 1) * P, :]).then_inc(adj_in[m], 16)
            with sp.Fori(0, B) as b:
                sp.wait_ge(out_ready, b + 1)
                sp.dma_start(out[bass.ds(b, 1)].rearrange("b (t p) c -> p (b t) c", p=P),
                             xb[:, bass.ds(b, 1)].rearrange("p b t c -> p (b t) c")
                             ).then_inc(out_done, 16)
            sp.wait_ge(out_done, 16 * B)

        @block.gpsimd
        def _(pool):
            nc.gpsimd.memset(ident_f[:], 1.0).then_inc(eye_set, 1)
            pool.wait_ge(eye_set, 1)
            nc.gpsimd.affine_select(out=ident_f[:], in_=ident_f[:], compare_op=ALU.is_equal, fill=0.0,
                                    base=0, pattern=[[-1, P]], channel_multiplier=1).then_inc(eye_set, 1)

        @block.tensor
        def _(pe):
            def product(dst, stat, mov, start, stop):
                pe.matmul(dst, stat(HI), mov(HI), start=start, stop=False)
                pe.matmul(dst, stat(HI), mov(LO), start=False, stop=False)
                return pe.matmul(dst, stat(LO), mov(HI), start=False, stop=stop)

            def adj_by(dst, src, half, tile_ready=None):
                for m in range(MT):
                    if tile_ready is not None:
                        tile_ready(m)
                    last = product(dst, lambda i: src(i, m),
                                   lambda i: adj[:, i, m, half * BANK:(half + 1) * BANK], m == 0, m == MT - 1)
                return last

            def pair_products(it, first=False):
                waited = [-A_PRE]

                def lo_reached(n):
                    if n > waited[0]:
                        waited[0] = n
                        pe.wait_ge(a_lo, it * A_LO_PAIR + (A_PRE + n))

                def bank_free(q):
                    lo_reached(a_lo_of(q - BANKS))

                for j in range(2):
                    q = j * A_MM
                    if j == 1:
                        lo_reached(a_lo_of(A1 + P1 + A2 - 1) + 1)
                    elif first:
                        lo_reached(1 - A_PRE)
                    if first and j == 0:
                        for m in range(MT):
                            lo_reached(1 + (m + 1) + (m >= W1_AT) - A_PRE)
                            for half in range(HALVES):
                                last = product(ps[:, half, :], lambda i: node[:, i, m * P:(m + 1) * P],
                                               lambda i: adj[:, i, m, half * BANK:(half + 1) * BANK],
                                               m == 0, m == MT - 1)
                                if m == MT - 1:
                                    last.then_inc(a_mm, 1)
                        q += HALVES
                    else:
                        for half in range(HALVES):
                            bank_free(q)
                            adj_by(ps[:, q % BANKS, :], lambda i, m: node[:, i, m * P:(m + 1) * P],
                                   half).then_inc(a_mm, 1)
                            q += 1
                    lo_reached(0)
                    per = BANK // H1
                    for u in range(P1):
                        bank_free(q)
                        lo_reached(a_lo_of(j * A_MM + u * per * P // BANK))
                        for t in range(per):
                            nt = (u * per + t) * P
                            last = product(ps[:, q % BANKS, t * H1:(t + 1) * H1],
                                           lambda i: y1[:, i, nt:nt + P], lambda i: w1s[:, i, :], True, True)
                        last.then_inc(a_mm, 1)
                        q += 1
                    h1_unit = j * A_MM + A1
                    for half in range(HALVES):
                        for k in range(K2):
                            bank_free(q)

                            def h1_ready(m):
                                lo_reached(a_lo_of(h1_unit + m // per))
                            adj_by(ps[:, q % BANKS, :], lambda i, m: h1[:, i, m, k * P:(k + 1) * P], half,
                                   h1_ready if half == 0 and k == 0 else None).then_inc(a_mm, 1)
                            q += 1
                    y2_unit = h1_unit + P1
                    for half in range(HALVES):
                        lo_reached(a_lo_of(y2_unit + (half + 1) * K2 - 1))
                        for g in range(K3):
                            bank_free(q)
                            for k in range(K2):
                                last = product(ps[:, q % BANKS, :], lambda i: w2s[:, i, k, g * P:(g + 1) * P],
                                               lambda i: y2[:, i, k, half * BANK:(half + 1) * BANK],
                                               k == 0, k == K2 - 1)
                            last.then_inc(a_mm, 1)
                            q += 1
                    h2_unit = y2_unit + A2
                    for u in range(P3):
                        bank_free(q)
                        half = u * 2 * P // BANK
                        lo_reached(a_lo_of(h2_unit + (half + 1) * K3 - 1))
                        for t in range(2):
                            nt = (2 * u + t) * P
                            for k in range(K3):
                                pe.matmul(ps[:, q % BANKS, 2 * t * F:(2 * t + 2) * F], h2[:, HI, k, nt:nt + P],
                                          w3s[:, k, :, :].rearrange("p a c -> p (a c)"),
                                          start=(k == 0), stop=False, skip_group_check=True)
                                last = pe.matmul(ps[:, q % BANKS, 2 * t * F:(2 * t + 1) * F],
                                                 h2[:, LO, k, nt:nt + P], w3s[:, k, HI, :],
                                                 start=False, stop=(k == K3 - 1), skip_group_check=True)
                        last.then_inc(a_mm, 1)
                        q += 1
                for m in range(MT):
                    lo_reached(a_lo_of(2 * A_MM - A3 + m // 2))
                    for u in range(A3):
                        if m == 0:
                            bank_free(q + u)
                        for t in range(2):
                            nt = (2 * u + t) * P
                            dst = ps[:, (q + u) % BANKS, 2 * t * F:(2 * t + 2) * F]
                            for a, b in ((HI, HI), (HI, LO), (LO, HI)):
                                last = pe.matmul(dst, adj[:, a, m, nt:nt + P],
                                                 s3[:, b, m, :, :].rearrange("p j c -> p (j c)"),
                                                 start=(m == 0 and t == 0 and (a, b) == (HI, HI)),
                                                 stop=(m == MT - 1 and a == LO), skip_group_check=True)
                        if m == MT - 1:
                            last.then_inc(a_mm, 1)
                    if m < MT - 1:
                        last.then_inc(adj_used, 1)

            pair_products(0, first=True)
            with pe.Fori(1, PAIRS) as it:
                pair_products(it)

            pe.wait_ge(const_set, 1)
            for m in range(MT):
                pe.wait_ge(b_lo, m + 1)
                for half in range(HALVES):
                    for i in (HI, LO):
                        last = pe.matmul(ps[:, half, :], ones[:], adj[:, i, m, half * BANK:(half + 1) * BANK],
                                         start=(m == 0 and i == HI), stop=(m == MT - 1 and i == LO))
            last.then_inc(b_mm, 1)

            def add_bias(dst, stat, mov):
                return pe.matmul(dst, stat, mov, start=False, stop=True)

            def pe_slot(slot, turn):
                waited = [-1]

                def lo_reached(n):
                    if n > waited[0]:
                        waited[0] = n
                        pe.wait_ge(b_lo, ahead("lo", slot, turn, B_PRE + n))

                def bank_free(r):
                    if r >= 2:
                        lo_reached(b_lo_of(r - 2))
                    elif slot > LOOP0 or turn is not None:
                        pe.wait_ge(fin_add, ahead("fin", slot, turn, FIN_PRE + r - 1 if slot > LOOP0 else FIN_PRE))

                def mm_unit(r):
                    return ps[:, GB + r % 2, :]

                if slot == 0:
                    pe.wait_ge(a_lo, A_PRE + PAIRS * A_LO_PAIR)
                if 0 < slot < B:
                    lo_reached(0)
                k, gate, n_fin, begun = 0, 0, 0, False
                for item in items(slot):
                    if isinstance(item, Step) or item[0] == "ahead":
                        u = steps_of(slot)[k]
                        if slot == 1 and k == 0:
                            pe.wait_ge(lw_lo, LW)
                        cols = columns(u, u.n)
                        src = h0 if u.p == 1 else ht[:, :, (slot - u.back) % 2, :]
                        names = gates_of(u.s)
                        reads = needs(slot, k)

                        def gate_bank(a):
                            return ps[:, (AHEAD["gate"][slot] + gate + a) % GB, 0:u.n]

                        def gate_bank_free(a):
                            n = gate + a + 1 - GB
                            if AHEAD["gate"][slot] + n > 0:
                                pe.wait_ge(gate_act, ahead("gate", slot, turn, n))

                        def h_ready():
                            pe.wait_ge(h_done, ahead("unit", slot, turn, k - reads + 1))

                        if u.s == 0 and u.p > 1:
                            h_ready()
                        for a, g in () if begun else enumerate(names):
                            if a in (0, 2):
                                gate_bank_free(min(a + 1, len(names) - 1))
                            last = product(gate_bank(a), lambda i: lw[:, i, u.p - 1, g * F:(g + 1) * F],
                                           lambda i: src[:, i, cols], True, u.s == 0)
                            if u.s == 0:
                                last.then_inc(gate_mm, 1)
                        begun = item[0] == "ahead"
                        if begun:
                            continue
                        if u.s > 0:
                            h_ready()
                            for a, g in enumerate(names):
                                product(gate_bank(a), lambda i: lw[:, i, whh(u.p), g * F:(g + 1) * F],
                                        lambda i: hstep[:, i, u.stream, 0:u.n], False,
                                        True).then_inc(gate_mm, 1)
                        k, gate = k + 1, gate + len(names)
                    elif item[0] == "adj_x":
                        half = item[1]
                        bank_free(half)
                        adj_by(mm_unit(half), lambda i, m: node[:, i, m * P:(m + 1) * P],
                               half).then_inc(b_mm, 1)
                    elif item[0] == "wg0":
                        v = item[1]
                        bank_free(2 + v)
                        lo_reached(b_lo_of(v))
                        for t in range(4):
                            nt = (4 * v + t) * P
                            dst = mm_unit(2 + v)[:, t * F:(t + 1) * F]
                            product(dst, lambda i: z[:, i, nt:nt + P], lambda i: wgs[:, i, 0, :], True, False)
                            last = add_bias(dst, rowsum[:, nt:nt + P], brow[:, 0, :])
                        last.then_inc(b_mm, 1)
                    elif item[0] == "adj_h":
                        _, half, m0, m1 = item
                        if m0 == 0:
                            bank_free(4 + half)
                        for m in range(m0, m1):
                            lo_reached(b_lo_of(2 + m // 4))
                            last = product(mm_unit(4 + half), lambda i: node[:, i, m * P:(m + 1) * P],
                                           lambda i: adj[:, i, m, half * BANK:(half + 1) * BANK],
                                           m == 0, m == MT - 1)
                        if m1 == MT:
                            last.then_inc(b_mm, 1)
                    elif item[0] == "wg1":
                        half = item[1]
                        bank_free(6 + half)
                        lo_reached(b_lo_of(4 + half))
                        cols = slice(half * BANK, (half + 1) * BANK)
                        product(mm_unit(half), lambda i: wgs[:, i, 1, :], lambda i: z[:, i, cols],
                                True, False)
                        add_bias(mm_unit(half), brow[:, 1, :], rowsum[:, cols]).then_inc(b_mm, 1)
                    elif item[0] == "fin":
                        _, v, back = item
                        if v == 0:
                            last_step = before(slot, k, lambda w, b: b + w.back == back and w.p == SKIPS
                                               and w.s == SKIPS - 1)
                            pe.wait_ge(h_done, ahead("unit", slot, turn, k - last_step + 1))
                        if slot < B:
                            lo_reached(b_lo_of(6 + v))
                        else:
                            pe.wait_ge(fin_add, ahead("fin", slot, turn, FIN_PRE + n_fin - 1))
                        for t in range(4):
                            nt = (4 * v + t) * P
                            dst = mm_unit(v)[:, t * F:(t + 1) * F]
                            pe.matmul(dst, ht[:, HI, (slot - back) % 2, nt:nt + P], ident[:], start=True, stop=False)
                            last = pe.matmul(dst, ht[:, LO, (slot - back) % 2, nt:nt + P], ident[:],
                                             start=False, stop=True)
                        last.then_inc(fin_mm, 1)
                        n_fin += 1

            slots(pe, pe_slot)

        @block.scalar
        def _(act):
            def x_hi(batch, done):
                src = xb[:, batch:batch + 1] if isinstance(batch, int) else xb[:, bass.ds(batch, 1)]
                nc.scalar.activation(node[:, HI, :], src.rearrange("p b t c -> p (b t c)"),
                                     ACT.Copy).then_inc(done, 1)

            act.wait_ge(x0_in, 16)
            nc.scalar.activation(node[:, HI, :], xb[:, 0].rearrange("p t c -> p (t c)"),
                                 ACT.Copy).then_inc(a_hi, 1)
            for m in range(MT):
                if m == W1_AT:
                    act.wait_ge(w1_in, 16)
                    nc.scalar.activation(w1s[:, HI, :], w0_raw[:, 0:H1], ACT.Copy).then_inc(a_hi, 1)
                if m % 2:
                    act.wait_ge(adj_in[m], 16)
                    nc.scalar.activation(square[:, m, :], square[:, m, :], ACT.Square).then_inc(sq_act, 1)
                    act.wait_ge(sq_act, m // 2 + 1)
                else:
                    act.wait_ge(sq_done, m // 2 + 1)
                nc.scalar.activation(adj[:, HI, m, :], square[:, m, :], ACT.Copy).then_inc(a_hi, 1)
            act.wait_ge(w0_in, 32)
            nc.scalar.activation(w2s[:, HI, :, :].rearrange("p k g -> p (k g)"), w0_raw[:, H1:H1 + K2 * H2],
                                 ACT.Copy)
            nc.scalar.activation(w3s[:, :, HI, :], w0_raw[:, H1 + K2 * H2:].rearrange("p (k g) -> p k g", k=K3),
                                 ACT.Copy).then_inc(a_hi, 1)

            with act.Fori(0, PAIRS) as it:
                for j in range(2):
                    mm0 = it * A_MM_PAIR + j * A_MM
                    q = 0

                    def hi_part(dst, func):
                        act.wait_ge(a_mm, mm0 + (q + 1))
                        nc.scalar.activation(dst, ps[:, (j * A_MM + q) % BANKS, :], func).then_inc(a_hi, 1)

                    for half in range(HALVES):
                        hi_part(y1[:, HI, half * BANK:(half + 1) * BANK], ACT.Copy)
                        q += 1
                    for u in range(P1):
                        hi_part(h1[:, HI, 2 * u:2 * u + 2, :].rearrange("p t g -> p (t g)"), ACT.Relu)
                        q += 1
                    for half in range(HALVES):
                        for k in range(K2):
                            hi_part(y2[:, HI, k, half * BANK:(half + 1) * BANK], ACT.Copy)
                            q += 1
                    act.wait_ge(xr_in, 16 * (B - 1))
                    x_hi((it * 2 + (j + 1)) % B, a_hi)
                    for half in range(HALVES):
                        for g in range(K3):
                            hi_part(h2[:, HI, g, half * BANK:(half + 1) * BANK], ACT.Relu)
                            q += 1
                    for u in range(P3):
                        act.wait_ge(a_mm, mm0 + (q + 1))
                        if u >= 2:
                            act.wait_ge(a_lo, it * A_LO_PAIR + (A_PRE + a_lo_of(j * A_MM + q - 2)))
                        nc.scalar.activation(
                            cross[:, u % 2], ps[:, (j * A_MM + q) % BANKS, :].rearrange(
                                "p (t a c) -> p t a c", t=2, a=2)[:, :, 1, :], ACT.Copy).then_inc(a_hi, 1)
                        q += 1

            for m in range(MT):
                act.wait_ge(adj_in[m], 32)
                if m < MT - 1:
                    act.wait_ge(adj_used, (PAIRS - 1) * (MT - 1) + (m + 1))
                else:
                    act.wait_ge(a_mm, PAIRS * A_MM_PAIR)
                nc.scalar.activation(adj[:, HI, m, :], adj_raw[:, m, :], ACT.Copy).then_inc(b_hi, 1)
            act.wait_ge(b_mm, 1)
            nc.scalar.activation(h0[:, HI, :], ps[:, 0:2, :].rearrange("p a c -> p (a c)"),
                                 ACT.Copy).then_inc(b_hi, 1)

            def act_slot(slot, turn):
                def hi_part(r, dst, func):
                    act.wait_ge(b_mm, ahead("mm", slot, turn, 1 + r + 1))
                    nc.scalar.activation(dst, ps[:, GB + r % 2, :], func).then_inc(b_hi, 1)

                k, gate = 0, 0
                for item in items(slot):
                    if isinstance(item, Step):
                        u = item
                        at = slice(0, u.n)
                        back = place_before(slot, k)
                        if back is not None:
                            act.wait_ge(h_done, ahead("unit", slot, turn, k - back + 1))
                        for g in gates_of(u.s):
                            act.wait_ge(gate_mm, ahead("gate", slot, turn, gate + 1))
                            col = (u.p - 1) * 4 + g
                            nc.scalar.activation(gates[:, u.stream, g, at],
                                                 ps[:, (AHEAD["gate"][slot] + gate) % GB, 0:u.n],
                                                 ACT.Tanh if g == GG else ACT.Sigmoid,
                                                 bias=lb[:, col:col + 1]).then_inc(gate_act, 1)
                            gate += 1
                        act.wait_ge(cell_done, ahead("unit", slot, turn, k + 1))
                        nc.scalar.activation(gates[:, u.stream, GG, at], gates[:, u.stream, 4, at],
                                             ACT.Tanh).then_inc(tanh_done, 1)
                        k += 1
                        continue
                    if item[0] == "weights":
                        act.wait_ge(lw_in, 16 * 8)
                        act.wait_ge(b_lo, MT)
                        for i in range(LW):
                            nc.scalar.activation(lw[:, HI, i, :], lw_raw[:, i, :], ACT.Copy).then_inc(lw_hi, 1)
                    cols = None if len(item) == 1 else slice(item[1] * BANK, (item[1] + 1) * BANK)
                    if item[0] == "adj_x":
                        hi_part(item[1], z[:, HI, cols], ACT.Copy)
                    elif item[0] == "wg0":
                        hi_part(2 + item[1], node[:, HI, cols], ACT.Relu)
                    elif item[0] == "adj_h" and item[3] == MT:
                        hi_part(4 + item[1], z[:, HI, cols], ACT.Copy)
                    elif item[0] == "split":
                        x_hi(batch_of(slot, turn, -1) % B, b_hi)
                    elif item[0] == "wg1":
                        hi_part(6 + item[1], h0[:, HI, cols], ACT.Relu)

            slots(act, act_slot)

        @block.vector
        def _(dve):

            def lo_part(dst, src, hi, done):
                nc.vector.tensor_tensor(dst, src, f32(hi), ALU.subtract).then_inc(done, 1)

            def lo_relu(dst, src, hi, done):
                nc.vector.scalar_tensor_tensor(out=dst, in0=src, scalar=0.0, in1=f32(hi), op0=ALU.max,
                                               op1=ALU.subtract).then_inc(done, 1)

            def pick(b, n):
                return slice(b, b + n) if isinstance(b, int) else bass.ds(b, n)

            def x_lo(batch, done):
                src = xb[:, batch:batch + 1] if isinstance(batch, int) else xb[:, bass.ds(batch, 1)]
                lo_part(node[:, LO, :], src.rearrange("p b t c -> p (b t c)"), node[:, HI, :], done)

            def group_stats(groups, at):
                nc.vector.memset(took_wait[:, 0:1], 0.0)
                for g, rows in groups:
                    last = nc.vector.bn_stats(stats[:, g, :], rows)
                last.then_inc(ln_step, 1)
                dve.wait_ge(ln_step, at + 1)
                nc.vector.memset(took_wait[:, 1:2], 0.0)
                for g, _ in groups:
                    last = nc.vector.bn_aggr(mv[:, g, :], stats[:, g, :])
                last.then_inc(ln_step, 1)

            def inverse_root(groups, at):
                g0, g1 = groups[0][0], groups[-1][0] + 1
                v, y, t = (newton[:, i, g0:g1] for i in range(3))
                as_int = lambda ap: ap.bitcast(I32)
                dve.wait_ge(ln_step, at + 2)
                nc.vector.tensor_scalar(v, mv[:, g0:g1, 1], EPS, None, ALU.add).then_inc(ln_step, 1)
                dve.wait_ge(ln_step, at + 3)
                nc.vector.tensor_scalar(as_int(t), as_int(v), 1, None,
                                        ALU.logical_shift_right).then_inc(ln_step, 1)
                dve.wait_ge(ln_step, at + 4)
                nc.vector.tensor_scalar(as_int(y), as_int(t), -1.0, float(0x5F3759DF), ALU.mult,
                                        ALU.add).then_inc(ln_step, 1)
                for i in range(NEWTON):
                    dve.wait_ge(ln_step, at + (5 + 3 * i))
                    nc.vector.scalar_tensor_tensor(out=t, in0=y, scalar=-0.5, in1=v, op0=ALU.mult,
                                                   op1=ALU.mult).then_inc(ln_step, 1)
                    dve.wait_ge(ln_step, at + (5 + 3 * i + 1))
                    nc.vector.tensor_tensor(t, t, y, ALU.mult).then_inc(ln_step, 1)
                    dve.wait_ge(ln_step, at + (5 + 3 * i + 2))
                    nc.vector.scalar_tensor_tensor(out=y, in0=t, scalar=1.5, in1=y, op0=ALU.add,
                                                   op1=ALU.mult).then_inc(ln_step, 1)

            def scale_rows(groups, at, done):
                dve.wait_ge(ln_step, at + LN_STEPS)
                for g, rows in groups:
                    last = nc.vector.tensor_scalar(rows, rows, mv[:, g, 0:1], newton[:, 1, g:g + 1],
                                                   ALU.subtract, ALU.mult)
                last.then_inc(done, 1)


            def square_tile(m):
                dve.wait_ge(adj_in[m], 16)
                nc.vector.tensor_tensor(square[:, m, :], square[:, m, :], square[:, m, :],
                                        ALU.mult).then_inc(sq_done, 1)

            square_tile(0)
            dve.wait_ge(a_hi, 1)
            lo_part(node[:, LO, :], xb[:, 0].rearrange("p t c -> p (t c)"), node[:, HI, :], a_lo)
            for m in range(MT):
                if m % 2 and m + 1 < MT:
                    square_tile(m + 1)
                if m == W1_AT:
                    dve.wait_ge(a_hi, 1 + m + 1)
                    lo_part(w1s[:, LO, :], w0_raw[:, 0:H1], w1s[:, HI, :], a_lo)
                dve.wait_ge(a_hi, 1 + (m + 1) + (m >= W1_AT))
                lo_part(adj[:, LO, m, :], square[:, m, :], adj[:, HI, m, :], a_lo)
            dve.wait_ge(a_hi, A_PRE)
            nc.vector.tensor_tensor(w2s[:, LO, :, :].rearrange("p k g -> p (k g)"), w0_raw[:, H1:H1 + K2 * H2],
                                    f32(w2s[:, HI, :, :]).rearrange("p k g -> p (k g)"), ALU.subtract)
            lo_part(w3s[:, :, LO, :], w0_raw[:, H1 + K2 * H2:].rearrange("p (k g) -> p k g", k=K3),
                    w3s[:, :, HI, :], a_lo)

            A_OWN = 2 * (2 * P3)
            def pair(it, first=False):
                own0 = it * A_OWN + own_pre
                if not first:
                    pair_sums(it - 1)
                    pair_stats(it - 1)
                for j in range(2):
                    hi0 = it * A_HI_PAIR + (A_PRE + j * A_LO)
                    q = 0
                    n_hi = 0

                    def bank():
                        return ps[:, (j * A_MM + q) % BANKS, :]

                    def hi_ready():
                        dve.wait_ge(a_hi, hi0 + (n_hi + 1))

                    for half in range(HALVES):
                        hi_ready()
                        cols = slice(half * BANK, (half + 1) * BANK)
                        lo_part(y1[:, LO, cols], bank(), y1[:, HI, cols], a_lo)
                        q, n_hi = q + 1, n_hi + 1
                        if half == 0 and j == 0 and not first:
                            inverse_root(pair_rows(it - 1), (it - 1) * LN_STEPS)
                    for u in range(P1):
                        hi_ready()
                        lo_relu(h1[:, LO, 2 * u:2 * u + 2, :].rearrange("p t g -> p (t g)"), bank(),
                                h1[:, HI, 2 * u:2 * u + 2, :].rearrange("p t g -> p (t g)"), a_lo)
                        q, n_hi = q + 1, n_hi + 1
                    if j == 0 and not first:
                        scale_rows(pair_rows(it - 1), (it - 1) * LN_STEPS, a_ln)
                    for half in range(HALVES):
                        for k in range(K2):
                            hi_ready()
                            cols = slice(half * BANK, (half + 1) * BANK)
                            lo_part(y2[:, LO, k, cols], bank(), y2[:, HI, k, cols], a_lo)
                            q, n_hi = q + 1, n_hi + 1
                    hi_ready()
                    x_lo((it * 2 + (j + 1)) % B, a_lo)
                    n_hi += 1
                    for half in range(HALVES):
                        for g in range(K3):
                            hi_ready()
                            cols = slice(half * BANK, (half + 1) * BANK)
                            lo_relu(h2[:, LO, g, cols], bank(), h2[:, HI, g, cols], a_lo)
                            q, n_hi = q + 1, n_hi + 1
                    for u in range(P3):
                        own_at = own0 + (j * 2 * P3 + 2 * u)
                        hi_ready()
                        if u > 0:
                            dve.wait_ge(a_lo, it * A_LO_PAIR + (A_PRE + a_lo_of(j * A_MM + q - 1)))
                        nc.vector.tensor_tensor(
                            s3full[:], bank().rearrange("p (t a c) -> p t a c", t=2, a=2)[:, :, 0, :],
                            cross[:, u % 2], ALU.add).then_inc(own, 1)
                        dve.wait_ge(own, own_at + 1)
                        nc.vector.tensor_copy(s3[:, HI, 2 * u:2 * u + 2, j, :], s3full[:]).then_inc(own, 1)
                        dve.wait_ge(own, own_at + 2)
                        lo_part(s3[:, LO, 2 * u:2 * u + 2, j, :], s3full[:],
                                s3[:, HI, 2 * u:2 * u + 2, j, :], a_lo)
                        q, n_hi = q + 1, n_hi + 1

            def pair_sums(it):
                for u in range(A3):
                    q = 2 * A_MM + u
                    dve.wait_ge(a_mm, it * A_MM_PAIR + (q + 1))
                    rows = xb[:, pick(it * 2, 2), 2 * u:2 * u + 2, :]
                    nc.vector.tensor_tensor(rows, rows, ps[:, q % BANKS, :].rearrange(
                        "p (t j c) -> p j t c", t=2, j=2), ALU.add).then_inc(a_lo, 1)

            def pair_rows(it):
                return [(MT * j + t, xb[:, pick(it * 2 + j, 1), t, :].rearrange("p b c -> p (b c)"))
                        for j in range(2) for t in range(MT)]

            def pair_stats(it):
                dve.wait_ge(a_lo, it * A_LO_PAIR + (A_PRE + A_LO_PAIR))
                group_stats(pair_rows(it), it * LN_STEPS)

            own_pre = 0
            pair(0, first=True)
            nc.vector.memset(sel[:], 0.0).then_inc(own, 1)
            dve.wait_ge(own, A_OWN + 1)
            for row, col in ((0, 0), (32, 0), (64, 1), (0, 2), (64, 2), (32, 3)):
                nc.vector.memset(sel[row:row + 1, col:col + 1], 1.0)
            dve.wait_ge(lw_in, 16 * 8)
            nc.vector.tensor_tensor(lb[:], lb_raw[:, 0, :], lb_raw[:, 1, :], ALU.add)
            nc.vector.tensor_copy(wgs[:, HI, :, :], wg_raw[:, 0:2, :])
            nc.vector.tensor_copy(bparts[:, HI, :, :], wg_raw[:, 2:4, :]).then_inc(own, 1)
            dve.wait_ge(own, A_OWN + 2)
            nc.vector.tensor_tensor(wgs[:, LO, :, :], wg_raw[:, 0:2, :], f32(wgs[:, HI, :, :]), ALU.subtract)
            nc.vector.tensor_tensor(bparts[:, LO, :, :], wg_raw[:, 2:4, :], f32(bparts[:, HI, :, :]),
                                    ALU.subtract)
            nc.vector.tensor_scalar(brow[:], f32(bparts[:, HI, :, :]), sel[:, 2:3], None,
                                    ALU.mult).then_inc(own, 1)
            dve.wait_ge(own, A_OWN + 3)
            nc.vector.scalar_tensor_tensor(out=brow[:].rearrange("p a c -> p (a c)"),
                                           in0=f32(bparts[:, LO, :, :]).rearrange("p a c -> p (a c)"),
                                           scalar=sel[:, 3:4], in1=f32(brow[:]).rearrange("p a c -> p (a c)"),
                                           op0=ALU.mult, op1=ALU.add)
            dve.wait_ge(eye_set, 2)
            nc.vector.tensor_copy(ident[:], ident_f[:]).then_inc(own, 1)
            dve.wait_ge(own, A_OWN + 4)
            nc.vector.memset(ident_f[:], 1.0).then_inc(own, 1)
            dve.wait_ge(own, A_OWN + 5)
            nc.vector.tensor_copy(ones[:], ident_f[:]).then_inc(const_set, 1)
            own_pre = 5

            with dve.Fori(1, PAIRS) as it:
                pair(it)
            for m in range(MT):
                dve.wait_ge(b_hi, m + 1)
                lo_part(adj[:, LO, m, :], adj_raw[:, m, :], adj[:, HI, m, :], b_lo)
            pair_sums(PAIRS - 1)
            own_pre += PAIRS * A_OWN
            dve.wait_ge(b_hi, MT + 1)
            nc.vector.tensor_tensor(h0[:, LO, :], ps[:, 0:2, :].rearrange("p a c -> p (a c)"),
                                    f32(h0[:, HI, :]), ALU.subtract)
            nc.vector.tensor_scalar(rowsum[:], f32(h0[:, HI, :]), sel[:, 0:1], None,
                                    ALU.mult).then_inc(own, 1)
            dve.wait_ge(own, own_pre + 1)
            nc.vector.scalar_tensor_tensor(out=rowsum[:], in0=f32(h0[:, LO, :]), scalar=sel[:, 1:2],
                                           in1=f32(rowsum[:]), op0=ALU.mult, op1=ALU.add).then_inc(b_lo, 1)
            dve.wait_ge(b_lo, MT + 1)
            for i in (HI, LO):
                last = nc.vector.memset(f32(ht[:, i, :, N:HTW]), 0.0)
            last.then_inc(fin_add, 1)

            def dve_slot(slot, turn):
                def hi_ready(n):
                    dve.wait_ge(b_hi, ahead("lo", slot, turn, B_PRE + n))

                k, gate, n_cell, n_fin, n_norm = 0, 0, 0, 0, 0
                for item in items(slot):
                    if isinstance(item, Step):
                        u = item

                        def work(g, n=u.n):
                            return gates[:, u.stream, g, 0:n]

                        def step_reached(n):
                            dve.wait_ge(cell_step, ahead("cell", slot, turn, n_cell + n))

                        dve.wait_ge(gate_act, ahead("gate", slot, turn, gate + 2))
                        if u.s == 0:
                            nc.vector.tensor_tensor(work(4), work(GI), work(GG), ALU.mult).then_inc(cell_done, 1)
                            used = 0
                        else:
                            nc.vector.tensor_tensor(work(GI), work(GI), work(GG), ALU.mult).then_inc(cell_step, 1)
                            dve.wait_ge(gate_act, ahead("gate", slot, turn, gate + 3))
                            nc.vector.tensor_tensor(work(GF), work(GF), work(4), ALU.mult).then_inc(cell_step, 1)
                            step_reached(2)
                            nc.vector.tensor_tensor(work(4), work(GI), work(GF), ALU.add).then_inc(cell_done, 1)
                            used = 2
                        if u.s == u.p - 1:
                            n = u.nw
                            to = ht[:, :, (slot - u.back) % 2, columns(u, n)]
                        else:
                            n = u.n
                            to = hstep[:, :, u.stream, 0:n]
                        dve.wait_ge(tanh_done, ahead("unit", slot, turn, k + 1))
                        h = work(GO, n)
                        nc.vector.tensor_tensor(h, h, work(GG, n), ALU.mult).then_inc(cell_step, 1)
                        step_reached(used + 1)
                        nc.vector.tensor_copy(to[:, HI], h).then_inc(cell_step, 1)
                        step_reached(used + 2)
                        lo_part(to[:, LO], h, to[:, HI], h_done)
                        k, gate, n_cell = k + 1, gate + len(gates_of(u.s)), n_cell + used + 2
                        continue
                    if item[0] == "weights":
                        for i in range(LW):
                            dve.wait_ge(lw_hi, i + 1)
                            lo_part(lw[:, LO, i, :], lw_raw[:, i, :], lw[:, HI, i, :], lw_lo)
                    if item[0] == "pair_stats":
                        pair_stats(PAIRS - 1)
                        inverse_root(pair_rows(PAIRS - 1), (PAIRS - 1) * LN_STEPS)
                    if item[0] == "pair_scale":
                        scale_rows(pair_rows(PAIRS - 1), (PAIRS - 1) * LN_STEPS, a_ln)
                    cols = None if len(item) == 1 else slice(item[1] * BANK, (item[1] + 1) * BANK)
                    if item[0] == "adj_x":
                        hi_ready(item[1] + 1)
                        lo_part(z[:, LO, cols], ps[:, GB + item[1], :], z[:, HI, cols], b_lo)
                    elif item[0] == "wg0":
                        hi_ready(2 + item[1] + 1)
                        lo_relu(node[:, LO, cols], ps[:, GB + item[1], :], node[:, HI, cols], b_lo)
                    elif item[0] == "adj_h" and item[3] == MT:
                        hi_ready(4 + item[1] + 1)
                        lo_part(z[:, LO, cols], ps[:, GB + item[1], :], z[:, HI, cols], b_lo)
                    elif item[0] == "split":
                        hi_ready(7)
                        x_lo(batch_of(slot, turn, -1) % B, b_lo)
                    elif item[0] == "wg1":
                        hi_ready(8 + item[1])
                        lo_relu(h0[:, LO, cols], ps[:, GB + item[1], :], h0[:, HI, cols], b_lo)
                    elif item[0] == "fin":
                        _, v, back = item
                        dve.wait_ge(fin_mm, ahead("fin", slot, turn, n_fin + 1))
                        rows = xb[:, pick(batch_of(slot, turn, back), 1), 4 * v:4 * v + 4, :].rearrange(
                            "p b t c -> p (b t c)")
                        nc.vector.tensor_tensor(rows, rows, ps[:, GB + v, :], ALU.add).then_inc(fin_add, 1)
                        n_fin += 1
                    elif item[0] in ("stats", "norm"):
                        b = batch_of(slot, turn, item[1])
                        groups = [(t, xb[:, pick(b, 1), t, :].rearrange("p b c -> p (b c)")) for t in range(MT)]
                        at = ahead("norm", slot, turn, (PAIRS + n_norm) * LN_STEPS)
                        if item[0] == "stats":
                            dve.wait_ge(fin_add, ahead("fin", slot, turn, FIN_PRE + n_fin))
                            group_stats(groups, at)
                        else:
                            inverse_root(groups, at)
                            scale_rows(groups, at, out_ready)
                            n_norm += 1

            slots(dve, dve_slot)


def kernel(x, adj, L0_gnn_W1, L0_gnn_W2, L0_gnn_W3, L1_gnn_Wg0, L1_gnn_bg0, L1_gnn_Wg1, L1_gnn_bg1,
           L1_gnn_Wih, L1_gnn_Whh, L1_gnn_bih, L1_gnn_bhh):
    import concourse.bacc as bacc
    from concourse.bass_utils import run_bass_kernel_spmd

    def rows(b):
        return np.broadcast_to(b, (P, b.shape[0]))

    def per_feature(b):
        return np.asarray(b).reshape(SKIPS, 4, P).transpose(2, 0, 1).reshape(P, SKIPS * 4)

    host = {
        "x": x, "adj_t": np.asarray(adj).T, "w1": L0_gnn_W1, "w2": L0_gnn_W2, "w3": L0_gnn_W3,
        "wg0": L1_gnn_Wg0, "bg0": rows(np.asarray(L1_gnn_bg0)), "wg1": L1_gnn_Wg1,
        "bg1": rows(np.asarray(L1_gnn_bg1)), "wih_t": np.asarray(L1_gnn_Wih).transpose(0, 2, 1),
        "whh_t": np.asarray(L1_gnn_Whh).transpose(0, 2, 1), "bih": per_feature(L1_gnn_bih),
        "bhh": per_feature(L1_gnn_bhh),
    }
    nc = bacc.Bacc("TRN2", target_bir_lowering=False, num_devices=1)
    arrays, args = {}, []
    for name, a in host.items():
        a = np.ascontiguousarray(a)
        arrays[f"in_{name}"] = a
        args.append(nc.dram_tensor(f"in_{name}", a.shape, mybir.dt.from_np(a.dtype), kind="ExternalInput").ap())
    out = nc.dram_tensor("out_0", tuple(np.shape(x)), F32, kind="ExternalOutput").ap()
    build(nc, *args, out)
    r = run_bass_kernel_spmd(nc, [arrays], core_ids=[0])
    return r.results[0]["out_0"]
```

```python
from collections import namedtuple
from contextlib import ExitStack

import numpy as np

import concourse.bass as bass
import concourse.mybir as mybir

F32 = mybir.dt.float32
F32R = mybir.dt.float32r
I32 = mybir.dt.int32
ALU = mybir.AluOpType
ACT = mybir.ActivationFunctionType

P = 128
BANK = 512
BANKS = 8
HI, LO = 0, 1
EPS = 1e-5
NEWTON = 3
LN_STEPS = 2 + 3 + 3 * NEWTON
SKIPS = 4
GI, GF, GG, GO = range(4)


def build(nc, x, adj_t, w1, w2, w3, wg0, bg0, wg1, bg1, wih_t, whh_t, bih, bhh, out):
    B, N, F = x.shape
    H1, H2 = w1.shape[1], w2.shape[1]
    MT = N // P
    HALVES = N // BANK
    K2, K3 = H1 // P, H2 // P
    PAIRS = B // 2
    G4 = SKIPS * P
    assert F == P and HALVES == 2 and w3.shape[1] == F and wih_t.shape == (SKIPS, F, 4 * F)

    ctx = ExitStack()
    with ctx:
        base = (nc.sbuf_base + 63) // 64 * 64
        top = [base]

        def place(nbytes):
            at = top[0]
            top[0] += (nbytes + 63) // 64 * 64
            return at

        def sb(name, shape, dt, at=None):
            size = 4 * int(np.prod(shape[1:]))
            return nc.alloc_sbuf_tensor_at(name, shape, dt, offset=place(size) if at is None else at)

        KB = 1024
        adj_at = place(2 * MT * N * 4)
        adj = sb("adj", [P, 2, MT, N], F32R, adj_at)
        square = sb("square", [P, MT, N], F32, adj_at + MT * N * 4)
        xb = sb("xb", [P, B, MT, F], F32)
        node = sb("node", [P, 2, N], F32R)
        big_at = place(32 * KB)
        y1 = sb("y1", [P, 2, N], F32R, big_at)
        h1 = sb("h1", [P, 2, MT, H1], F32R, big_at + 8 * KB)
        h2 = sb("h2", [P, 2, K3, N], F32R, big_at)
        adj_raw = sb("adj_raw", [P, MT, N], F32, big_at)
        lw = sb("lw", [P, 2, 2 * SKIPS - 1, G4], F32R, big_at)
        rowsum = sb("rowsum", [P, N], F32R, big_at + 28 * KB)
        r2_at = place(16 * KB)
        y2 = sb("y2", [P, 2, K2, N], F32R, r2_at)
        w0_raw = sb("w0_raw", [P, H1 + K2 * H2 + K3 * F], F32, r2_at)
        tile_sum = sb("tile_sum", [P, N], F32, r2_at + 4 * N)
        z = sb("z", [P, 2, N], F32R, r2_at)
        hs_at = r2_at + 8 * KB
        HTW = N + 2
        h0 = sb("h0", [P, 2, N], F32R, hs_at)
        r3_at = place(16 * KB)
        s3 = sb("s3", [P, 2, MT, 2, F], F32R, r3_at)
        w0_at = place(4 * 2 * (H1 + K2 * H2 + K3 * F))
        w1s = sb("w1s", [P, 2, H1], F32R, w0_at)
        w2s = sb("w2s", [P, 2, K2, H2], F32R, w0_at + 8 * H1)
        w3s = sb("w3s", [P, K3, 2, F], F32R, w0_at + 8 * (H1 + K2 * H2))
        lw_raw_at = place(4 * (2 * SKIPS - 1) * G4 + 64)
        lw_raw = sb("lw_raw", [P, 2 * SKIPS - 1, G4], F32, lw_raw_at)
        ht = sb("ht", [P, 2, 2, HTW], F32R, r3_at)
        gates_at = (r3_at + 4 * 4 * HTW + 63) // 64 * 64
        gates = sb("gates", [P, 2, 5, BANK], F32, gates_at)
        hstep = sb("hstep", [P, 2, 2, BANK], F32R, gates_at + 4 * 10 * BANK)
        ht_last = sb("ht_last", [P, 2, HTW], F32R, adj_at)
        gates_last = sb("gates_last", [P, 5, BANK], F32, adj_at + 12 * KB)
        hstep_last = sb("hstep_last", [P, 2, BANK], F32R, adj_at + 12 * KB + 4 * 5 * BANK)
        assert gates_at + 4 * 14 * BANK <= lw_raw_at + 4 * (2 * SKIPS - 1) * G4 + 64
        wg_raw_at = place(2 * KB)
        wg_raw = sb("wg_raw", [P, 4, F], F32, wg_raw_at)
        wgs = sb("wgs", [P, 2, 2, F], F32R)
        cross_at = place(2 * KB)
        cross = sb("cross", [P, 2, 2, F], F32, cross_at)
        bparts = sb("bparts", [P, 2, 2, F], F32R, cross_at)
        bias0 = [sb("bias0_a", [P, BANK], F32, cross_at), sb("bias0_b", [P, BANK], F32, wg_raw_at)]
        brow = sb("brow", [P, 2, F], F32R)
        ident_f = sb("ident_f", [P, P], F32)
        ident = sb("ident", [P, P], F32R)
        ones = sb("ones", [P, P], F32R)
        lb_raw = sb("lb_raw", [P, 2, SKIPS * 4], F32)
        lb = sb("lb", [P, SKIPS * 4], F32)
        sel = sb("sel", [P, 4], F32)
        s3full = sb("s3full", [P, 2, F], F32)
        stats = sb("stats", [P, 16, 6], F32)
        mv = sb("mv", [P, 16, 2], F32)
        took_wait = sb("took_wait", [P, 2], F32)
        newton = sb("newton", [P, 3, 16], F32)
        assert top[0] <= nc.sbuf_usable_end

        ps = ctx.enter_context(nc.psum_tensor("ps", [P, BANKS, BANK], F32))

        def sem(name):
            return ctx.enter_context(nc.semaphore(name))

        x0_in = sem("x0_in")
        xr_in = sem("xr_in")
        adj_in = [sem(f"adj_in{m}") for m in range(MT)]
        w1_in = sem("w1_in")
        w0_in = sem("w0_in")
        lw_in = sem("lw_in")
        eye_set = sem("eye_set")
        const_set = sem("const_set")
        own = sem("own")
        ln_step = sem("ln_step")
        cell_step = sem("cell_step")
        sq_done = sem("sq_done")
        sq_act = sem("sq_act")
        adj_used = sem("adj_used")
        a_mm, a_hi, a_lo = sem("a_mm"), sem("a_hi"), sem("a_lo")
        a_ln = sem("a_ln")
        b_mm, b_hi, b_lo = sem("b_mm"), sem("b_hi"), sem("b_lo")
        acc_step = sem("acc_step")
        acc_hi, acc_lo = sem("acc_hi"), sem("acc_lo")
        sum_mm, sum_hi, sum_lo = sem("sum_mm"), sem("sum_hi"), sem("sum_lo")
        bias_mm, bias_set = sem("bias_mm"), sem("bias_set")
        bias_add = sem("bias_add")
        lw_hi, lw_lo = sem("lw_hi"), sem("lw_lo")
        gate_mm = sem("gate_mm")
        gate_act = sem("gate_act")
        cell_done = sem("cell_done")
        tanh_done = sem("tanh_done")
        h_done = sem("h_done")
        fin_mm = sem("fin_mm")
        fin_add = sem("fin_add")
        shift_set = sem("shift_set")
        out_ready = sem("out_ready")
        half_ready = sem("half_ready")
        out_done = sem("out_done")

        A1, P1, A2, P2, P3, A3 = HALVES, MT * H1 // BANK, HALVES * K2, HALVES * K3, MT // 2, MT // 2
        A_MM = A1 + P1 + A2 + P2 + P3
        A_LO = A_MM + 1
        A_MM_PAIR, A_LO_PAIR = 2 * A_MM + A3, 2 * A_LO + A3
        A_HI_PAIR = 2 * A_LO
        A_PRE = 1 + MT + 2
        W1_AT = 5
        assert A_MM_PAIR % BANKS == 0

        def a_lo_of(q):
            if q < 0:
                return a_lo_of(q + A_MM_PAIR) - A_LO_PAIR
            if q >= 2 * A_MM:
                return 2 * A_LO + (q - 2 * A_MM) + 1
            j, r = divmod(q, A_MM)
            return j * A_LO + r + 1 + (r >= A1 + P1 + A2)

        LW = 2 * SKIPS - 1
        B_PRE = MT
        ADDED = 7
        B_MM = 8
        GB = 6

        def splits(slot):
            return slot < B - 1

        def b_lo_of(slot, r):
            return r + 1 + (r >= 6 and splits(slot))

        Step = namedtuple("Step", "stream p s w0 nw n back held")
        X, Y, Z = 0, 1, 2

        def step(stream, p, s, w0=0, back=None, nw=None, held=False):
            nw = nw or min(N // p, BANK)
            return Step(stream, p, s, w0, nw, nw + nw % 2, (2 if stream == X else 1) if back is None else back,
                        held)

        def finished_by(item, begun):
            begun.append(item)
            last = len(begun) - item.held
            ended, begun[:] = begun[:last], begun[last:]
            return ended

        SLOT = [step(Y, 1, 0), ("stats", 3), ("adj_x", 0, 0, 8), ("ahead",), step(X, 3, 0),
                ("adj_x", 1, 0, 8), step(X, 3, 1), ("wg0", 0), ("wg0", 1), ("ahead",), step(X, 3, 2),
                ("adj_h", 0, 0, 4), ("adj_h", 0, 4, 8), ("ahead",), step(X, 4, 0), ("ahead",),
                step(Y, 1, 0, BANK), ("ahead",), step(X, 4, 1), ("ahead",), ("adj_h", 1, 0, 6),
                ("root", 3), step(X, 4, 2), ("adj_h", 1, 6, 8), ("split",), ("wg1", 0), ("ahead",),
                step(X, 4, 3, held=True), ("ahead",), step(Y, 2, 0), ("wg1", 1), ("scale", 3),
                ("ahead",), ("fin", 0, 2), step(Y, 2, 1), ("fin", 1, 2)]
        DRAIN = [("adj_x", 0, 0, 4), step(Y, 1, 0, held=True), step(X, 3, 0), ("adj_x", 0, 4, 8),
                ("ahead",), ("adj_x", 1, 0, 4), step(Y, 1, 0, BANK), ("adj_x", 1, 4, 8),
                step(Y, 2, 0, held=True), ("stats", 3), ("ahead",), ("wg0", 0), ("wg0", 1),
                step(X, 3, 1), ("adj_h", 0, 0, 6), ("root", 3), ("scale", 3), step(Y, 2, 1, held=True),
                ("ahead",), ("adj_h", 0, 6, 8), step(X, 3, 2), ("adj_h", 1, 0, 8), ("wg1", 0),
                step(X, 4, 0), ("wg1", 1), step(Y, 3, 0, held=True), step(X, 4, 1)]
        LAST = [step(Z, 1, 0), step(Y, 3, 1, back=2, held=True), step(Z, 1, 0, BANK),
                step(X, 4, 2, back=3, held=True), step(Y, 3, 2, back=2, held=True), step(Z, 2, 0),
                step(X, 4, 3, back=3), step(Z, 2, 1, held=True), step(Y, 4, 0, back=2), ("fin", 0, 3),
                ("ahead",), step(Z, 3, 0), ("fin", 1, 3), ("ahead",), ("stats", 3),
                step(Z, 3, 1, held=True), step(Y, 4, 1, back=2, held=True), ("root", 3), step(Z, 3, 2),
                ("ahead",), step(Y, 4, 2, back=2, held=True), ("ahead",), step(Z, 4, 0), ("scale", 3),
                step(Y, 4, 3, back=2, held=True), step(Z, 4, 1), ("ahead",), ("fin", 0, 2),
                ("fin", 1, 2), ("stats", 2), step(Z, 4, 2), ("root", 2), step(Z, 4, 3), ("scale", 2),
                ("fin", 0, 1), ("part", 0, 1), ("fin", 1, 1), ("part", 1, 1), ("root", 1), ("scale", 1)]
        SLOTS = B + 1

        def items(slot):
            if slot == SLOTS - 1:
                return LAST
            full = DRAIN if slot == B - 1 else SLOT
            kept = []
            for i, item in enumerate(full):
                if item == ("ahead",):
                    back = next(u for u in full[i:] if isinstance(u, Step)).back
                elif isinstance(item, Step):
                    back = item.back
                else:
                    back = item[-1] if item[0] in ("fin", "stats", "root", "scale") else 0
                if slot < back:
                    continue
                if isinstance(item, Step) and slot == 1:
                    item = item._replace(held=False)
                kept.append(item)
                if slot == 0 and item[:2] == ("adj_x", 0) and item[3] == MT:
                    kept.append(("rowsum",))
                if slot == 0 and item[:2] == ("adj_x", 1) and item[3] == MT:
                    kept.append(("bias",))
                if slot == 0 and item == ("wg0", 1):
                    kept.append(("weights",))
                if slot == 0 and item == ("wg1", 1):
                    kept.append(("pair_stats",))
                if slot == 1 and isinstance(item, Step) and item[:3] == (Y, 2, 0):
                    kept.append(("pair_scale",))
            return kept

        def gates_of(s):
            return (GI, GG, GO) if s == 0 else (GI, GG, GF, GO)

        def steps_of(slot):
            return [item for item in items(slot) if isinstance(item, Step)]

        def count(slot, name):
            return sum(item[0] == name for item in items(slot) if not isinstance(item, Step))

        CELL_STEPS = (2, 4)
        PER_SLOT = {
            "mm": lambda n: B_MM * (n < B),
            "lo": lambda n: (B_MM + splits(n)) * (n < B),
            "bias": lambda n: 2 * (n < B),
            "gate": lambda n: sum(len(gates_of(u.s)) for u in steps_of(n)),
            "unit": lambda n: len(steps_of(n)),
            "cell": lambda n: sum(CELL_STEPS[u.s > 0] for u in steps_of(n)),
            "fin": lambda n: count(n, "fin"),
            "norm": lambda n: count(n, "scale") * LN_STEPS,
        }
        AHEAD = {k: [sum(f(m) for m in range(n)) for n in range(SLOTS + 1)] for k, f in PER_SLOT.items()}
        LOOP0 = 3
        TURNS = (B - 1 - LOOP0) // 2
        PER_TURN = {k: v[LOOP0 + 2] - v[LOOP0] for k, v in AHEAD.items()}
        assert PER_TURN["gate"] % GB == 0
        FIN_PRE = 2

        def ahead(what, slot, turn, more=0):
            n = AHEAD[what][slot] + more
            return n if turn is None else turn * PER_TURN[what] + n

        def batch_of(slot, turn, back):
            n = slot - back
            return n if turn is None else turn * 2 + n

        def slots(eng, body):
            for slot in range(LOOP0):
                body(slot, None)
            with eng.Fori(0, TURNS) as turn:
                for slot in (LOOP0, LOOP0 + 1):
                    body(slot, turn)
            for slot in range(LOOP0 + 2 * TURNS, SLOTS):
                body(slot, None)

        def before(slot, k, same):
            back, at = 0, k
            while True:
                own_steps = steps_of(slot - back)
                for i in range(at - 1, -1, -1):
                    if same(own_steps[i], back):
                        return sum(len(steps_of(slot - b)) for b in range(1, back + 1)) + k - i
                back += 1
                if slot - back < 1:
                    return None
                at = len(steps_of(slot - back))

        def needs(slot, k):
            u = steps_of(slot)[k]
            if u.s > 0:
                return before(slot, k, lambda v, b: b + v.back == u.back
                              and (v.p, v.s, v.w0) == (u.p, u.s - 1, u.w0))
            if u.p == 1:
                return None
            return before(slot, k, lambda v, b: b + v.back == u.back and (v.p, v.s) == (u.p - 1, u.p - 2))

        def span(u, n=None):
            at = u.w0 % BANK
            return slice(at, at + (n or u.n))

        def h_in(slot, back):
            return ht_last if slot - back == B - 1 else ht[:, :, (slot - back) % 2, :]

        def gates_in(stream):
            return gates_last if stream == Z else gates[:, stream]

        def hstep_in(stream):
            return hstep_last if stream == Z else hstep[:, :, stream]

        def place_before(slot, k):
            u = steps_of(slot)[k]
            return before(slot, k, lambda v, b: v.stream == u.stream and span(v).start < span(u).stop
                          and span(u).start < span(v).stop)

        def columns(u, nw):
            first = u.w0 * u.p + u.s
            return slice(first, first + u.p * (nw - 1) + 1, u.p)

        def loop_slot_steps_match():
            for slot in (LOOP0, LOOP0 + 1):
                for k in range(len(steps_of(slot))):
                    assert needs(slot, k) == needs(slot + 2, k)

        loop_slot_steps_match()

        def whh(p):
            return SKIPS + p - 2

        def f32(ap):
            return ap.bitcast(F32)

        block = ctx.enter_context(nc.Block())

        @block.sync
        def _(sp):
            for m in range(MT):
                if m == 1:
                    sp.dma_start(xb[:, 0], x[0].rearrange("(t p) c -> p t c", p=P)).then_inc(x0_in, 16)
                if m == W1_AT:
                    sp.dma_start(w0_raw[:, 0:H1], w1).then_inc(w1_in, 16)
                sp.dma_start(square[:, m, :], adj_t[m * P:(m + 1) * P, :]).then_inc(adj_in[m], 16)
            sp.dma_start(w0_raw[:, H1:H1 + K2 * H2].rearrange("p (k g) -> p k g", k=K2),
                         w2.rearrange("(k p) g -> p k g", p=P)).then_inc(w0_in, 16)
            sp.dma_start(w0_raw[:, H1 + K2 * H2:].rearrange("p (k g) -> p k g", k=K3),
                         w3.rearrange("(k p) g -> p k g", p=P)).then_inc(w0_in, 16)
            for b in range(1, B):
                sp.dma_start(xb[:, b], x[b].rearrange("(t p) c -> p t c", p=P)).then_inc(xr_in, 16)
            for k, small in enumerate((wg0, wg1, bg0, bg1)):
                sp.dma_start(wg_raw[:, k, :], small).then_inc(lw_in, 16)
            sp.dma_start(lb_raw[:, 0, :], bih).then_inc(lw_in, 16)
            sp.dma_start(lb_raw[:, 1, :], bhh).then_inc(lw_in, 16)
            sp.dma_start(lw_raw[:, 0:SKIPS, :], wih_t.rearrange("s f g -> f s g")).then_inc(lw_in, 16)
            sp.dma_start(lw_raw[:, SKIPS:, :], whh_t[1:].rearrange("s f g -> f s g")).then_inc(lw_in, 16)
            sp.wait_ge(a_mm, PAIRS * A_MM_PAIR - A3)
            for m in range(MT):
                sp.dma_start(adj_raw[:, m, :], adj_t[m * P:(m + 1) * P, :]).then_inc(adj_in[m], 16)
            with sp.Fori(0, B - 1) as b:
                sp.wait_ge(out_ready, b + 1)
                sp.dma_start(out[bass.ds(b, 1)].rearrange("b (t p) c -> p (b t) c", p=P),
                             xb[:, bass.ds(b, 1)].rearrange("p b t c -> p (b t) c")
                             ).then_inc(out_done, 16)
            for v, done in ((0, (out_ready, B)), (1, (half_ready, 1))):
                sp.wait_ge(*done)
                sp.dma_start(out[B - 1].rearrange("(t p) c -> p t c", p=P)[:, 4 * v:4 * v + 4, :],
                             xb[:, B - 1, 4 * v:4 * v + 4, :]).then_inc(out_done, 16)
            sp.wait_ge(out_done, 16 * (B + 1))

        @block.gpsimd
        def _(pool):
            nc.gpsimd.memset(ident_f[:], 1.0).then_inc(eye_set, 1)
            pool.wait_ge(eye_set, 1)
            nc.gpsimd.affine_select(out=ident_f[:], in_=ident_f[:], compare_op=ALU.is_equal, fill=0.0,
                                    base=0, pattern=[[-1, P]], channel_multiplier=1).then_inc(eye_set, 1)

        @block.tensor
        def _(pe):
            def product(dst, stat, mov, start, stop):
                pe.matmul(dst, stat(HI), mov(HI), start=start, stop=False)
                pe.matmul(dst, stat(HI), mov(LO), start=False, stop=False)
                return pe.matmul(dst, stat(LO), mov(HI), start=False, stop=stop)

            def adj_by(dst, src, half, m0=0, m1=MT, tile_ready=None):
                for m in range(m0, m1):
                    if tile_ready is not None:
                        tile_ready(m)
                    last = product(dst, lambda i: src(i, m),
                                   lambda i: adj[:, i, m, half * BANK:(half + 1) * BANK], m == 0, m == MT - 1)
                return last

            def pair_products(it, first=False):
                waited = [-A_PRE]

                def lo_reached(n):
                    if n > waited[0]:
                        waited[0] = n
                        pe.wait_ge(a_lo, it * A_LO_PAIR + (A_PRE + n))

                def bank_free(q):
                    lo_reached(a_lo_of(q - BANKS))

                for j in range(2):
                    q = j * A_MM
                    if j == 1:
                        lo_reached(a_lo_of(A1 + P1 + A2 - 1) + 1)
                    elif first:
                        lo_reached(1 - A_PRE)
                    if first and j == 0:
                        for m in range(MT):
                            lo_reached(1 + (m + 1) + (m >= W1_AT) - A_PRE)
                            for half in range(HALVES):
                                last = product(ps[:, half, :], lambda i: node[:, i, m * P:(m + 1) * P],
                                               lambda i: adj[:, i, m, half * BANK:(half + 1) * BANK],
                                               m == 0, m == MT - 1)
                                if m == MT - 1:
                                    last.then_inc(a_mm, 1)
                        q += HALVES
                    else:
                        for half in range(HALVES):
                            bank_free(q)
                            adj_by(ps[:, q % BANKS, :], lambda i, m: node[:, i, m * P:(m + 1) * P],
                                   half).then_inc(a_mm, 1)
                            q += 1
                    lo_reached(0)
                    per = BANK // H1
                    for u in range(P1):
                        bank_free(q)
                        lo_reached(a_lo_of(j * A_MM + u * per * P // BANK))
                        for t in range(per):
                            nt = (u * per + t) * P
                            last = product(ps[:, q % BANKS, t * H1:(t + 1) * H1],
                                           lambda i: y1[:, i, nt:nt + P], lambda i: w1s[:, i, :], True, True)
                        last.then_inc(a_mm, 1)
                        q += 1
                    h1_unit = j * A_MM + A1
                    for half in range(HALVES):
                        for k in range(K2):
                            bank_free(q)

                            def h1_ready(m):
                                lo_reached(a_lo_of(h1_unit + m // per))
                            adj_by(ps[:, q % BANKS, :], lambda i, m: h1[:, i, m, k * P:(k + 1) * P], half,
                                   tile_ready=h1_ready if half == 0 and k == 0 else None).then_inc(a_mm, 1)
                            q += 1
                    y2_unit = h1_unit + P1
                    for half in range(HALVES):
                        lo_reached(a_lo_of(y2_unit + (half + 1) * K2 - 1))
                        for g in range(K3):
                            bank_free(q)
                            for k in range(K2):
                                last = product(ps[:, q % BANKS, :], lambda i: w2s[:, i, k, g * P:(g + 1) * P],
                                               lambda i: y2[:, i, k, half * BANK:(half + 1) * BANK],
                                               k == 0, k == K2 - 1)
                            last.then_inc(a_mm, 1)
                            q += 1
                    h2_unit = y2_unit + A2
                    for u in range(P3):
                        bank_free(q)
                        half = u * 2 * P // BANK
                        lo_reached(a_lo_of(h2_unit + (half + 1) * K3 - 1))
                        for t in range(2):
                            nt = (2 * u + t) * P
                            for k in range(K3):
                                pe.matmul(ps[:, q % BANKS, 2 * t * F:(2 * t + 2) * F], h2[:, HI, k, nt:nt + P],
                                          w3s[:, k, :, :].rearrange("p a c -> p (a c)"),
                                          start=(k == 0), stop=False, skip_group_check=True)
                                last = pe.matmul(ps[:, q % BANKS, 2 * t * F:(2 * t + 1) * F],
                                                 h2[:, LO, k, nt:nt + P], w3s[:, k, HI, :],
                                                 start=False, stop=(k == K3 - 1), skip_group_check=True)
                        last.then_inc(a_mm, 1)
                        q += 1
                for m in range(MT):
                    lo_reached(a_lo_of(2 * A_MM - A3 + m // 2))
                    for u in range(A3):
                        if m == 0:
                            bank_free(q + u)
                        for t in range(2):
                            nt = (2 * u + t) * P
                            dst = ps[:, (q + u) % BANKS, 2 * t * F:(2 * t + 2) * F]
                            for a, b in ((HI, HI), (HI, LO), (LO, HI)):
                                last = pe.matmul(dst, adj[:, a, m, nt:nt + P],
                                                 s3[:, b, m, :, :].rearrange("p j c -> p (j c)"),
                                                 start=(m == 0 and t == 0 and (a, b) == (HI, HI)),
                                                 stop=(m == MT - 1 and a == LO), skip_group_check=True)
                        if m == MT - 1:
                            last.then_inc(a_mm, 1)
                    if m < MT - 1:
                        last.then_inc(adj_used, 1)

            pair_products(0, first=True)
            with pe.Fori(1, PAIRS) as it:
                pair_products(it)

            def bias_product(dst, stat, mov, start):
                return pe.matmul(dst, stat, mov, start=start, stop=True)

            def pe_slot(slot, turn):
                waited = [-1]

                def lo_reached(n):
                    if n > waited[0]:
                        waited[0] = n
                        pe.wait_ge(b_lo, ahead("lo", slot, turn, B_PRE + n))

                def bank_free(r):
                    if r >= 2:
                        lo_reached(b_lo_of(slot, r - 2))
                    elif slot == 0 and r == 1:
                        pe.wait_ge(a_lo, A_PRE + PAIRS * A_LO_PAIR)
                    elif slot >= 2:
                        pe.wait_ge(fin_add, ahead("fin", slot, turn, FIN_PRE + r - 1))

                def mm_unit(r):
                    return ps[:, GB + r % 2, :]

                if slot == 0:
                    pe.wait_ge(a_lo, A_PRE + PAIRS * A_LO_PAIR - 1)
                if 0 < slot < B:
                    lo_reached(0)
                k, gate, n_fin, begun = 0, 0, 0, False
                for item in items(slot):
                    if isinstance(item, Step) or item[0] == "ahead":
                        u = steps_of(slot)[k]
                        if slot == 1 and k == 0:
                            pe.wait_ge(lw_lo, LW)
                        if u.p == 1:
                            lo_reached(0)
                        cols = columns(u, u.n)
                        src = h0 if u.p == 1 else h_in(slot, u.back)
                        names = gates_of(u.s)
                        reads = needs(slot, k)

                        def gate_bank(a):
                            return ps[:, (AHEAD["gate"][slot] + gate + a) % GB, 0:u.n]

                        def gate_bank_free(a):
                            n = gate + a + 1 - GB
                            if AHEAD["gate"][slot] + n > 0:
                                pe.wait_ge(gate_act, ahead("gate", slot, turn, n))

                        def h_ready():
                            pe.wait_ge(h_done, ahead("unit", slot, turn, k - reads + 1))

                        if u.s == 0 and u.p > 1:
                            h_ready()
                        for a, g in () if begun else enumerate(names):
                            if a in (0, 2):
                                gate_bank_free(min(a + 1, len(names) - 1))
                            last = product(gate_bank(a), lambda i: lw[:, i, u.p - 1, g * F:(g + 1) * F],
                                           lambda i: src[:, i, cols], True, u.s == 0)
                            if u.s == 0:
                                last.then_inc(gate_mm, 1)
                        begun = item[0] == "ahead"
                        if begun:
                            continue
                        if u.s > 0:
                            h_ready()
                            for a, g in enumerate(names):
                                product(gate_bank(a), lambda i: lw[:, i, whh(u.p), g * F:(g + 1) * F],
                                        lambda i: hstep_in(u.stream)[:, i, span(u)], False,
                                        True).then_inc(gate_mm, 1)
                        k, gate = k + 1, gate + len(names)
                    elif item[0] == "adj_x":
                        _, half, m0, m1 = item
                        if m0 == 0:
                            bank_free(half)

                        def tile_split(m):
                            pe.wait_ge(b_lo, m + 1)
                        last = adj_by(mm_unit(half), lambda i, m: node[:, i, m * P:(m + 1) * P], half, m0, m1,
                                      tile_split if slot == 0 and half == 0 else None)
                        if m1 == MT:
                            last.then_inc(b_mm, 1)
                    elif item[0] == "wg0":
                        v = item[1]
                        bank_free(2 + v)
                        lo_reached(b_lo_of(slot, v))
                        for t in range(4):
                            nt = (4 * v + t) * P
                            dst = mm_unit(2 + v)[:, t * F:(t + 1) * F]
                            last = product(dst, lambda i: z[:, i, nt:nt + P], lambda i: wgs[:, i, 0, :],
                                           True, True)
                        last.then_inc(b_mm, 1)
                    elif item[0] == "rowsum":
                        pe.wait_ge(acc_lo, 1)
                        pe.wait_ge(const_set, 1)
                        for half in range(HALVES):
                            cols = slice(half * BANK, (half + 1) * BANK)
                            parts = [adj[:, i, m, cols] for m in range(ADDED, MT) for i in (HI, LO)]
                            parts += [h0[:, HI, cols], h0[:, LO, cols]]
                            for n, part in enumerate(parts):
                                last = pe.matmul(ps[:, half, :], ones[:], part, start=(n == 0),
                                                 stop=(n == len(parts) - 1))
                        last.then_inc(sum_mm, 1)
                    elif item[0] == "bias":
                        pe.wait_ge(sum_lo, 1)
                        for t in range(MT):
                            last = bias_product(ps[:, t // 4, t % 4 * F:(t % 4 + 1) * F],
                                                rowsum[:, t * P:(t + 1) * P], brow[:, 0, :], True)
                        last.then_inc(bias_mm, 1)
                    elif item[0] == "adj_h":
                        _, half, m0, m1 = item
                        if m0 == 0:
                            bank_free(4 + half)

                        def h_tile_ready(m):
                            lo_reached(b_lo_of(slot, 2 + m // 4))
                        last = adj_by(mm_unit(4 + half), lambda i, m: node[:, i, m * P:(m + 1) * P], half,
                                      m0, m1, h_tile_ready)
                        if m1 == MT:
                            last.then_inc(b_mm, 1)
                    elif item[0] == "wg1":
                        half = item[1]
                        bank_free(6 + half)
                        lo_reached(b_lo_of(slot, 4 + half))
                        cols = slice(half * BANK, (half + 1) * BANK)
                        product(mm_unit(half), lambda i: wgs[:, i, 1, :], lambda i: z[:, i, cols],
                                True, False)
                        bias_product(mm_unit(half), brow[:, 1, :], rowsum[:, cols], False).then_inc(b_mm, 1)
                    elif item[0] == "fin":
                        _, v, back = item
                        if v == 0:
                            last_step = before(slot, k, lambda w, b: b + w.back == back and w.p == SKIPS
                                               and w.s == SKIPS - 1)
                            pe.wait_ge(h_done, ahead("unit", slot, turn, k - last_step + 1))
                        if slot < B:
                            lo_reached(b_lo_of(slot, 6 + v))
                        else:
                            lo_reached(0)
                            pe.wait_ge(fin_add, ahead("fin", slot, turn, FIN_PRE + n_fin - 1))
                        for t in range(4):
                            nt = (4 * v + t) * P
                            dst = mm_unit(v)[:, t * F:(t + 1) * F]
                            pe.matmul(dst, h_in(slot, back)[:, HI, nt:nt + P], ident[:], start=True, stop=False)
                            last = pe.matmul(dst, h_in(slot, back)[:, LO, nt:nt + P], ident[:],
                                             start=False, stop=True)
                        last.then_inc(fin_mm, 1)
                        n_fin += 1

            slots(pe, pe_slot)

        @block.scalar
        def _(act):
            def x_hi(batch, done):
                src = xb[:, batch:batch + 1] if isinstance(batch, int) else xb[:, bass.ds(batch, 1)]
                nc.scalar.activation(node[:, HI, :], src.rearrange("p b t c -> p (b t c)"),
                                     ACT.Copy).then_inc(done, 1)

            act.wait_ge(x0_in, 16)
            nc.scalar.activation(node[:, HI, :], xb[:, 0].rearrange("p t c -> p (t c)"),
                                 ACT.Copy).then_inc(a_hi, 1)
            for m in range(MT):
                if m == W1_AT:
                    act.wait_ge(w1_in, 16)
                    nc.scalar.activation(w1s[:, HI, :], w0_raw[:, 0:H1], ACT.Copy).then_inc(a_hi, 1)
                if m % 2:
                    act.wait_ge(adj_in[m], 16)
                    nc.scalar.activation(square[:, m, :], square[:, m, :], ACT.Square).then_inc(sq_act, 1)
                    act.wait_ge(sq_act, m // 2 + 1)
                else:
                    act.wait_ge(sq_done, m // 2 + 1)
                nc.scalar.activation(adj[:, HI, m, :], square[:, m, :], ACT.Copy).then_inc(a_hi, 1)
            act.wait_ge(w0_in, 32)
            nc.scalar.activation(w2s[:, HI, :, :].rearrange("p k g -> p (k g)"), w0_raw[:, H1:H1 + K2 * H2],
                                 ACT.Copy)
            nc.scalar.activation(w3s[:, :, HI, :], w0_raw[:, H1 + K2 * H2:].rearrange("p (k g) -> p k g", k=K3),
                                 ACT.Copy).then_inc(a_hi, 1)

            with act.Fori(0, PAIRS) as it:
                for j in range(2):
                    mm0 = it * A_MM_PAIR + j * A_MM
                    q = 0

                    def hi_part(dst, func):
                        act.wait_ge(a_mm, mm0 + (q + 1))
                        nc.scalar.activation(dst, ps[:, (j * A_MM + q) % BANKS, :], func).then_inc(a_hi, 1)

                    for half in range(HALVES):
                        hi_part(y1[:, HI, half * BANK:(half + 1) * BANK], ACT.Copy)
                        q += 1
                    for u in range(P1):
                        hi_part(h1[:, HI, 2 * u:2 * u + 2, :].rearrange("p t g -> p (t g)"), ACT.Relu)
                        q += 1
                    for half in range(HALVES):
                        for k in range(K2):
                            hi_part(y2[:, HI, k, half * BANK:(half + 1) * BANK], ACT.Copy)
                            q += 1
                    act.wait_ge(xr_in, 16 * (B - 1))
                    x_hi((it * 2 + (j + 1)) % B, a_hi)
                    for half in range(HALVES):
                        for g in range(K3):
                            hi_part(h2[:, HI, g, half * BANK:(half + 1) * BANK], ACT.Relu)
                            q += 1
                    for u in range(P3):
                        act.wait_ge(a_mm, mm0 + (q + 1))
                        if u >= 2:
                            act.wait_ge(a_lo, it * A_LO_PAIR + (A_PRE + a_lo_of(j * A_MM + q - 2)))
                        nc.scalar.activation(
                            cross[:, u % 2], ps[:, (j * A_MM + q) % BANKS, :].rearrange(
                                "p (t a c) -> p t a c", t=2, a=2)[:, :, 1, :], ACT.Copy).then_inc(a_hi, 1)
                        q += 1

            for m in range(MT):
                act.wait_ge(adj_in[m], 32)
                if m < MT - 1:
                    act.wait_ge(adj_used, (PAIRS - 1) * (MT - 1) + (m + 1))
                else:
                    act.wait_ge(a_mm, PAIRS * A_MM_PAIR)
                nc.scalar.activation(adj[:, HI, m, :], adj_raw[:, m, :], ACT.Copy).then_inc(b_hi, 1)
            act.wait_ge(acc_step, ADDED - 1)
            nc.scalar.activation(h0[:, HI, :], tile_sum[:], ACT.Copy).then_inc(acc_hi, 1)

            def act_slot(slot, turn):
                def hi_part(r, dst, func):
                    act.wait_ge(b_mm, ahead("mm", slot, turn, r + 1))
                    nc.scalar.activation(dst, ps[:, GB + r % 2, :], func).then_inc(b_hi, 1)

                k, gate, begun, n_ended = 0, 0, [], 0
                for item in items(slot):
                    if isinstance(item, Step):
                        u = item
                        at = span(u)
                        back = place_before(slot, k)
                        if back is not None:
                            act.wait_ge(h_done, ahead("unit", slot, turn, k - back + 1))
                        for g in gates_of(u.s):
                            act.wait_ge(gate_mm, ahead("gate", slot, turn, gate + 1))
                            col = (u.p - 1) * 4 + g
                            nc.scalar.activation(gates_in(u.stream)[:, g, at],
                                                 ps[:, (AHEAD["gate"][slot] + gate) % GB, 0:u.n],
                                                 ACT.Tanh if g == GG else ACT.Sigmoid,
                                                 bias=lb[:, col:col + 1]).then_inc(gate_act, 1)
                            gate += 1
                        k += 1
                        for v in finished_by(u, begun):
                            act.wait_ge(cell_done, ahead("unit", slot, turn, n_ended + 1))
                            work = gates_in(v.stream)[:, :, span(v)]
                            nc.scalar.activation(work[:, GG], work[:, 4], ACT.Tanh).then_inc(tanh_done, 1)
                            n_ended += 1
                        continue
                    if item[0] == "weights":
                        act.wait_ge(lw_in, 16 * 8)
                        act.wait_ge(b_lo, MT)
                        for i in range(LW):
                            nc.scalar.activation(lw[:, HI, i, :], lw_raw[:, i, :], ACT.Copy).then_inc(lw_hi, 1)
                    cols = None if len(item) == 1 else slice(item[1] * BANK, (item[1] + 1) * BANK)
                    if item[0] == "adj_x" and item[3] == MT:
                        hi_part(item[1], z[:, HI, cols], ACT.Copy)
                    elif item[0] == "rowsum":
                        act.wait_ge(sum_mm, 1)
                        nc.scalar.activation(h0[:, HI, :], ps[:, 0:2, :].rearrange("p a c -> p (a c)"),
                                             ACT.Copy).then_inc(sum_hi, 1)
                    elif item[0] == "bias":
                        act.wait_ge(bias_mm, 1)
                        for v in range(2):
                            nc.scalar.activation(bias0[v][:], ps[:, v, :], ACT.Copy).then_inc(bias_set, 1)
                    elif item[0] == "wg0":
                        act.wait_ge(bias_add, ahead("bias", slot, turn, item[1] + 1))
                        nc.scalar.activation(node[:, HI, cols], ps[:, GB + item[1], :], ACT.Relu).then_inc(b_hi, 1)
                    elif item[0] == "adj_h" and item[3] == MT:
                        hi_part(4 + item[1], z[:, HI, cols], ACT.Copy)
                    elif item[0] == "split":
                        x_hi(batch_of(slot, turn, -1), b_hi)
                    elif item[0] == "wg1":
                        hi_part(6 + item[1], h0[:, HI, cols], ACT.Relu)

            slots(act, act_slot)
            act.wait_ge(shift_set, 1)
            for t in range(4, MT):
                last = nc.scalar.activation(xb[:, B - 1, t, :], xb[:, B - 1, t, :], ACT.Identity,
                                            bias=newton[:, 2, t:t + 1], scale=newton[:, 1, t:t + 1])
            last.then_inc(half_ready, 1)

        @block.vector
        def _(dve):

            def lo_part(dst, src, hi, done):
                nc.vector.tensor_tensor(dst, src, f32(hi), ALU.subtract).then_inc(done, 1)

            def lo_relu(dst, src, hi, done):
                nc.vector.scalar_tensor_tensor(out=dst, in0=src, scalar=0.0, in1=f32(hi), op0=ALU.max,
                                               op1=ALU.subtract).then_inc(done, 1)

            def pick(b, n):
                return slice(b, b + n) if isinstance(b, int) else bass.ds(b, n)

            def x_lo(batch, done):
                src = xb[:, batch:batch + 1] if isinstance(batch, int) else xb[:, bass.ds(batch, 1)]
                lo_part(node[:, LO, :], src.rearrange("p b t c -> p (b t c)"), node[:, HI, :], done)

            def row_stats(groups):
                nc.vector.memset(took_wait[:, 0:1], 0.0)
                for g, rows in groups:
                    last = nc.vector.bn_stats(stats[:, g, :], rows)
                return last

            def group_stats(groups, at, rows_last=None):
                (rows_last or row_stats(groups)).then_inc(ln_step, 1)
                dve.wait_ge(ln_step, at + 1)
                nc.vector.memset(took_wait[:, 1:2], 0.0)
                for g, _ in groups:
                    last = nc.vector.bn_aggr(mv[:, g, :], stats[:, g, :])
                last.then_inc(ln_step, 1)

            def inverse_root(groups, at):
                g0, g1 = groups[0][0], groups[-1][0] + 1
                v, y, t = (newton[:, i, g0:g1] for i in range(3))
                as_int = lambda ap: ap.bitcast(I32)
                dve.wait_ge(ln_step, at + 2)
                nc.vector.tensor_scalar(v, mv[:, g0:g1, 1], EPS, None, ALU.add).then_inc(ln_step, 1)
                dve.wait_ge(ln_step, at + 3)
                nc.vector.tensor_scalar(as_int(t), as_int(v), 1, None,
                                        ALU.logical_shift_right).then_inc(ln_step, 1)
                dve.wait_ge(ln_step, at + 4)
                nc.vector.tensor_scalar(as_int(y), as_int(t), -1.0, float(0x5F3759DF), ALU.mult,
                                        ALU.add).then_inc(ln_step, 1)
                for i in range(NEWTON):
                    dve.wait_ge(ln_step, at + (5 + 3 * i))
                    nc.vector.scalar_tensor_tensor(out=t, in0=y, scalar=-0.5, in1=v, op0=ALU.mult,
                                                   op1=ALU.mult).then_inc(ln_step, 1)
                    dve.wait_ge(ln_step, at + (5 + 3 * i + 1))
                    nc.vector.tensor_tensor(t, t, y, ALU.mult).then_inc(ln_step, 1)
                    dve.wait_ge(ln_step, at + (5 + 3 * i + 2))
                    nc.vector.scalar_tensor_tensor(out=y, in0=t, scalar=1.5, in1=y, op0=ALU.add,
                                                   op1=ALU.mult).then_inc(ln_step, 1)

            def scale_rows(groups, at, done):
                dve.wait_ge(ln_step, at + LN_STEPS)
                for g, rows in groups:
                    last = nc.vector.tensor_scalar(rows, rows, mv[:, g, 0:1], newton[:, 1, g:g + 1],
                                                   ALU.subtract, ALU.mult)
                last.then_inc(done, 1)


            def square_tile(m):
                dve.wait_ge(adj_in[m], 16)
                nc.vector.tensor_tensor(square[:, m, :], square[:, m, :], square[:, m, :],
                                        ALU.mult).then_inc(sq_done, 1)

            square_tile(0)
            dve.wait_ge(a_hi, 1)
            lo_part(node[:, LO, :], xb[:, 0].rearrange("p t c -> p (t c)"), node[:, HI, :], a_lo)
            for m in range(MT):
                if m % 2 and m + 1 < MT:
                    square_tile(m + 1)
                if m == W1_AT:
                    dve.wait_ge(a_hi, 1 + m + 1)
                    lo_part(w1s[:, LO, :], w0_raw[:, 0:H1], w1s[:, HI, :], a_lo)
                dve.wait_ge(a_hi, 1 + (m + 1) + (m >= W1_AT))
                lo_part(adj[:, LO, m, :], square[:, m, :], adj[:, HI, m, :], a_lo)
            dve.wait_ge(a_hi, A_PRE)
            nc.vector.tensor_tensor(w2s[:, LO, :, :].rearrange("p k g -> p (k g)"), w0_raw[:, H1:H1 + K2 * H2],
                                    f32(w2s[:, HI, :, :]).rearrange("p k g -> p (k g)"), ALU.subtract)
            lo_part(w3s[:, :, LO, :], w0_raw[:, H1 + K2 * H2:].rearrange("p (k g) -> p k g", k=K3),
                    w3s[:, :, HI, :], a_lo)

            A_OWN = 2 * (2 * P3)
            def pair(it, first=False):
                own0 = it * A_OWN + own_pre
                if not first:
                    pair_sums(it - 1)
                    pair_stats(it - 1)
                for j in range(2):
                    hi0 = it * A_HI_PAIR + (A_PRE + j * A_LO)
                    q = 0
                    n_hi = 0

                    def bank():
                        return ps[:, (j * A_MM + q) % BANKS, :]

                    def hi_ready():
                        dve.wait_ge(a_hi, hi0 + (n_hi + 1))

                    for half in range(HALVES):
                        hi_ready()
                        cols = slice(half * BANK, (half + 1) * BANK)
                        lo_part(y1[:, LO, cols], bank(), y1[:, HI, cols], a_lo)
                        q, n_hi = q + 1, n_hi + 1
                        if half == 0 and j == 0 and not first:
                            inverse_root(pair_rows(it - 1), (it - 1) * LN_STEPS)
                    for u in range(P1):
                        hi_ready()
                        lo_relu(h1[:, LO, 2 * u:2 * u + 2, :].rearrange("p t g -> p (t g)"), bank(),
                                h1[:, HI, 2 * u:2 * u + 2, :].rearrange("p t g -> p (t g)"), a_lo)
                        q, n_hi = q + 1, n_hi + 1
                    if j == 0 and not first:
                        scale_rows(pair_rows(it - 1), (it - 1) * LN_STEPS, a_ln)
                    for half in range(HALVES):
                        for k in range(K2):
                            hi_ready()
                            cols = slice(half * BANK, (half + 1) * BANK)
                            lo_part(y2[:, LO, k, cols], bank(), y2[:, HI, k, cols], a_lo)
                            q, n_hi = q + 1, n_hi + 1
                    hi_ready()
                    x_lo((it * 2 + (j + 1)) % B, a_lo)
                    n_hi += 1
                    for half in range(HALVES):
                        for g in range(K3):
                            hi_ready()
                            cols = slice(half * BANK, (half + 1) * BANK)
                            lo_relu(h2[:, LO, g, cols], bank(), h2[:, HI, g, cols], a_lo)
                            q, n_hi = q + 1, n_hi + 1
                    for u in range(P3):
                        own_at = own0 + (j * 2 * P3 + 2 * u)
                        hi_ready()
                        if u > 0:
                            dve.wait_ge(a_lo, it * A_LO_PAIR + (A_PRE + a_lo_of(j * A_MM + q - 1)))
                        nc.vector.tensor_tensor(
                            s3full[:], bank().rearrange("p (t a c) -> p t a c", t=2, a=2)[:, :, 0, :],
                            cross[:, u % 2], ALU.add).then_inc(own, 1)
                        dve.wait_ge(own, own_at + 1)
                        nc.vector.tensor_copy(s3[:, HI, 2 * u:2 * u + 2, j, :], s3full[:]).then_inc(own, 1)
                        dve.wait_ge(own, own_at + 2)
                        lo_part(s3[:, LO, 2 * u:2 * u + 2, j, :], s3full[:],
                                s3[:, HI, 2 * u:2 * u + 2, j, :], a_lo)
                        q, n_hi = q + 1, n_hi + 1

            def pair_sums(it):
                for u in range(A3):
                    q = 2 * A_MM + u
                    dve.wait_ge(a_mm, it * A_MM_PAIR + (q + 1))
                    rows = xb[:, pick(it * 2, 2), 2 * u:2 * u + 2, :]
                    nc.vector.tensor_tensor(rows, rows, ps[:, q % BANKS, :].rearrange(
                        "p (t j c) -> p j t c", t=2, j=2), ALU.add).then_inc(a_lo, 1)

            def pair_rows(it):
                return [(MT * j + t, xb[:, pick(it * 2 + j, 1), t, :].rearrange("p b c -> p (b c)"))
                        for j in range(2) for t in range(MT)]

            def pair_stats(it):
                dve.wait_ge(a_lo, it * A_LO_PAIR + (A_PRE + A_LO_PAIR))
                group_stats(pair_rows(it), it * LN_STEPS)

            own_pre = 0
            pair(0, first=True)
            nc.vector.memset(sel[:], 0.0).then_inc(own, 1)
            dve.wait_ge(own, A_OWN + 1)
            for row, col in ((0, 0), (32, 0), (64, 1), (0, 2), (64, 2), (32, 3)):
                nc.vector.memset(sel[row:row + 1, col:col + 1], 1.0)
            dve.wait_ge(lw_in, 16 * 8)
            nc.vector.tensor_tensor(lb[:], lb_raw[:, 0, :], lb_raw[:, 1, :], ALU.add)
            nc.vector.tensor_copy(wgs[:, HI, :, :], wg_raw[:, 0:2, :])
            nc.vector.tensor_copy(bparts[:, HI, :, :], wg_raw[:, 2:4, :]).then_inc(own, 1)
            dve.wait_ge(own, A_OWN + 2)
            nc.vector.tensor_tensor(wgs[:, LO, :, :], wg_raw[:, 0:2, :], f32(wgs[:, HI, :, :]), ALU.subtract)
            nc.vector.tensor_tensor(bparts[:, LO, :, :], wg_raw[:, 2:4, :], f32(bparts[:, HI, :, :]),
                                    ALU.subtract)
            nc.vector.tensor_scalar(brow[:], f32(bparts[:, HI, :, :]), sel[:, 2:3], None,
                                    ALU.mult).then_inc(own, 1)
            dve.wait_ge(own, A_OWN + 3)
            nc.vector.scalar_tensor_tensor(out=brow[:].rearrange("p a c -> p (a c)"),
                                           in0=f32(bparts[:, LO, :, :]).rearrange("p a c -> p (a c)"),
                                           scalar=sel[:, 3:4], in1=f32(brow[:]).rearrange("p a c -> p (a c)"),
                                           op0=ALU.mult, op1=ALU.add)
            dve.wait_ge(eye_set, 2)
            nc.vector.tensor_copy(ident[:], ident_f[:]).then_inc(own, 1)
            dve.wait_ge(own, A_OWN + 4)
            nc.vector.memset(ident_f[:], 1.0).then_inc(own, 1)
            dve.wait_ge(own, A_OWN + 5)
            nc.vector.tensor_copy(ones[:], ident_f[:]).then_inc(const_set, 1)
            own_pre = 5

            with dve.Fori(1, PAIRS) as it:
                pair(it)
            for m in range(MT):
                for n in range(1 if m == 0 else m + 2, min(m + 3, ADDED)):
                    dve.wait_ge(adj_in[n], 32)
                    if n > 1:
                        dve.wait_ge(acc_step, n - 1)
                    nc.vector.tensor_tensor(tile_sum[:], adj_raw[:, 0, :] if n == 1 else tile_sum[:],
                                            adj_raw[:, n, :], ALU.add).then_inc(acc_step, 1)
                if m == MT - 1:
                    pair_sums(PAIRS - 1)
                dve.wait_ge(b_hi, m + 1)
                lo_part(adj[:, LO, m, :], adj_raw[:, m, :], adj[:, HI, m, :], b_lo)
            dve.wait_ge(acc_hi, 1)
            lo_part(h0[:, LO, :], tile_sum[:], h0[:, HI, :], acc_lo)
            own_pre += PAIRS * A_OWN
            for i in (HI, LO):
                nc.vector.memset(f32(ht[:, i, :, N:HTW]), 0.0).then_inc(fin_add, 1)
            dve.wait_ge(acc_lo, 1)

            def dve_slot(slot, turn):
                def hi_ready(n):
                    dve.wait_ge(b_hi, ahead("lo", slot, turn, B_PRE + n))

                gate, n_cell, n_fin, n_norm, begun, n_ended = 0, 0, 0, 0, [], 0

                def in_place(u, g, n=None):
                    return gates_in(u.stream)[:, g, span(u, n)]

                def step_reached(n):
                    dve.wait_ge(cell_step, ahead("cell", slot, turn, n))

                for item in items(slot):
                    if isinstance(item, Step):
                        u = item

                        def work(g):
                            return in_place(u, g)

                        dve.wait_ge(gate_act, ahead("gate", slot, turn, gate + 2))
                        if u.stream == Z and (u.p, u.w0) == (1, 0):
                            nc.vector.memset(f32(ht_last[:, :, N:HTW]), 0.0)
                        if u.s == 0:
                            nc.vector.tensor_tensor(work(4), work(GI), work(GG), ALU.mult).then_inc(cell_done, 1)
                        else:
                            nc.vector.tensor_tensor(work(GI), work(GI), work(GG), ALU.mult).then_inc(cell_step, 1)
                            dve.wait_ge(gate_act, ahead("gate", slot, turn, gate + 3))
                            nc.vector.tensor_tensor(work(GF), work(GF), work(4), ALU.mult).then_inc(cell_step, 1)
                            n_cell += 2
                            step_reached(n_cell)
                            nc.vector.tensor_tensor(work(4), work(GI), work(GF), ALU.add).then_inc(cell_done, 1)
                        gate += len(gates_of(u.s))
                        for v in finished_by(u, begun):
                            if v.s == v.p - 1:
                                n = v.nw
                                to = h_in(slot, v.back)[:, :, columns(v, n)]
                            else:
                                n = v.n
                                to = hstep_in(v.stream)[:, :, span(v)]
                            dve.wait_ge(tanh_done, ahead("unit", slot, turn, n_ended + 1))
                            h = in_place(v, GO, n)
                            nc.vector.tensor_tensor(h, h, in_place(v, GG, n), ALU.mult).then_inc(cell_step, 1)
                            step_reached(n_cell + 1)
                            nc.vector.tensor_copy(to[:, HI], h).then_inc(cell_step, 1)
                            step_reached(n_cell + 2)
                            lo_part(to[:, LO], h, to[:, HI], h_done)
                            n_cell, n_ended = n_cell + 2, n_ended + 1
                        continue
                    if item[0] == "weights":
                        for i in range(LW):
                            dve.wait_ge(lw_hi, i + 1)
                            lo_part(lw[:, LO, i, :], lw_raw[:, i, :], lw[:, HI, i, :], lw_lo)
                    if item[0] == "pair_stats":
                        pair_stats(PAIRS - 1)
                        inverse_root(pair_rows(PAIRS - 1), (PAIRS - 1) * LN_STEPS)
                    if item[0] == "pair_scale":
                        scale_rows(pair_rows(PAIRS - 1), (PAIRS - 1) * LN_STEPS, a_ln)
                    cols = None if len(item) == 1 else slice(item[1] * BANK, (item[1] + 1) * BANK)
                    if item[0] == "adj_x" and item[3] == MT:
                        hi_ready(item[1] + 1)
                        lo_part(z[:, LO, cols], ps[:, GB + item[1], :], z[:, HI, cols], b_lo)
                    elif item[0] == "rowsum":
                        dve.wait_ge(sum_hi, 1)
                        nc.vector.tensor_tensor(h0[:, LO, :], ps[:, 0:2, :].rearrange("p a c -> p (a c)"),
                                                f32(h0[:, HI, :]), ALU.subtract)
                        nc.vector.tensor_scalar(rowsum[:], f32(h0[:, HI, :]), sel[:, 0:1], None,
                                                ALU.mult).then_inc(own, 1)
                        dve.wait_ge(own, own_pre + 1)
                        nc.vector.scalar_tensor_tensor(
                            out=rowsum[:], in0=f32(h0[:, LO, :]), scalar=sel[:, 1:2], in1=f32(rowsum[:]),
                            op0=ALU.mult, op1=ALU.add).then_inc(sum_lo, 1)
                    elif item[0] == "wg0":
                        if slot == 0:
                            dve.wait_ge(bias_set, 1 + item[1])
                        dve.wait_ge(b_mm, ahead("mm", slot, turn, 2 + item[1] + 1))
                        unit = ps[:, GB + item[1], :]
                        nc.vector.tensor_tensor(unit, unit, bias0[item[1]][:], ALU.add).then_inc(bias_add, 1)
                        hi_ready(2 + item[1] + 1)
                        lo_relu(node[:, LO, cols], ps[:, GB + item[1], :], node[:, HI, cols], b_lo)
                    elif item[0] == "adj_h" and item[3] == MT:
                        hi_ready(4 + item[1] + 1)
                        lo_part(z[:, LO, cols], ps[:, GB + item[1], :], z[:, HI, cols], b_lo)
                    elif item[0] == "split":
                        hi_ready(7)
                        x_lo(batch_of(slot, turn, -1), b_lo)
                    elif item[0] == "wg1":
                        hi_ready(7 + splits(slot) + item[1])
                        lo_relu(h0[:, LO, cols], ps[:, GB + item[1], :], h0[:, HI, cols], b_lo)
                    elif item[0] == "fin":
                        _, v, back = item
                        dve.wait_ge(fin_mm, ahead("fin", slot, turn, n_fin + 1))
                        rows = xb[:, pick(batch_of(slot, turn, back), 1), 4 * v:4 * v + 4, :].rearrange(
                            "p b t c -> p (b t c)")
                        nc.vector.tensor_tensor(rows, rows, ps[:, GB + v, :], ALU.add).then_inc(fin_add, 1)
                        n_fin += 1
                    elif item[0] in ("stats", "root", "scale", "part"):
                        b = batch_of(slot, turn, item[-1])
                        groups = [(t, xb[:, pick(b, 1), t, :].rearrange("p b c -> p (b c)")) for t in range(MT)]
                        at = ahead("norm", slot, turn, (PAIRS + n_norm) * LN_STEPS)
                        if item[0] == "stats":
                            dve.wait_ge(fin_add, ahead("fin", slot, turn, FIN_PRE + n_fin))
                            group_stats(groups, at)
                        elif item[0] == "part":
                            v = item[1]
                            dve.wait_ge(fin_add, ahead("fin", slot, turn, FIN_PRE + n_fin))
                            last = row_stats(groups[4 * v:4 * v + 4])
                            if v == 1:
                                group_stats(groups, at, last)
                        elif item[0] == "root":
                            inverse_root(groups, at)
                        elif slot - item[1] == B - 1:
                            dve.wait_ge(ln_step, at + LN_STEPS)
                            nc.vector.scalar_tensor_tensor(
                                out=newton[:, 2, 4:MT], in0=mv[:, 4:MT, 0], scalar=-1.0, in1=newton[:, 1, 4:MT],
                                op0=ALU.mult, op1=ALU.mult).then_inc(shift_set, 1)
                            scale_rows(groups[0:4], at, out_ready)
                        else:
                            scale_rows(groups, at, out_ready)
                            n_norm += 1

            slots(dve, dve_slot)


def kernel(x, adj, L0_gnn_W1, L0_gnn_W2, L0_gnn_W3, L1_gnn_Wg0, L1_gnn_bg0, L1_gnn_Wg1, L1_gnn_bg1,
           L1_gnn_Wih, L1_gnn_Whh, L1_gnn_bih, L1_gnn_bhh):
    import concourse.bacc as bacc
    from concourse.bass_utils import run_bass_kernel_spmd

    def rows(b):
        return np.broadcast_to(b, (P, b.shape[0]))

    def per_feature(b):
        return np.asarray(b).reshape(SKIPS, 4, P).transpose(2, 0, 1).reshape(P, SKIPS * 4)

    host = {
        "x": x, "adj_t": np.asarray(adj).T, "w1": L0_gnn_W1, "w2": L0_gnn_W2, "w3": L0_gnn_W3,
        "wg0": L1_gnn_Wg0, "bg0": rows(np.asarray(L1_gnn_bg0)), "wg1": L1_gnn_Wg1,
        "bg1": rows(np.asarray(L1_gnn_bg1)), "wih_t": np.asarray(L1_gnn_Wih).transpose(0, 2, 1),
        "whh_t": np.asarray(L1_gnn_Whh).transpose(0, 2, 1), "bih": per_feature(L1_gnn_bih),
        "bhh": per_feature(L1_gnn_bhh),
    }
    nc = bacc.Bacc("TRN2", target_bir_lowering=False, num_devices=1)
    arrays, args = {}, []
    for name, a in host.items():
        a = np.ascontiguousarray(a)
        arrays[f"in_{name}"] = a
        args.append(nc.dram_tensor(f"in_{name}", a.shape, mybir.dt.from_np(a.dtype), kind="ExternalInput").ap())
    out = nc.dram_tensor("out_0", tuple(np.shape(x)), F32, kind="ExternalOutput").ap()
    build(nc, *args, out)
    r = run_bass_kernel_spmd(nc, [arrays], core_ids=[0])
    return r.results[0]["out_0"]
```
